# Optimizing a Trainium2 kernel written in Bass

```python
import numpy as np
import jax
import jax.numpy as jnp

def _softmax(x, axis=-1):
    return jax.nn.softmax(x, axis=axis)

def _gelu(x):
    return jax.nn.gelu(x, approximate=True)

def _silu(x):
    return jax.nn.silu(x)

def _sigmoid(x):
    return jax.nn.sigmoid(x)

def _layernorm(x, axis=-1, eps=1e-05):
    m = jnp.mean(x, axis=axis, keepdims=True)
    v = jnp.var(x, axis=axis, keepdims=True)
    return (x - m) / jnp.sqrt(v + eps)

def _scatter_add(tgt, idx, src, axis=0):
    return tgt.at[idx].add(src)

def _segment_sum(src, seg, n):
    return jax.ops.segment_sum(src, seg, n)
kernel_name = 'mk_lm_tower_d1_tok_ids256_r4_a6d926'

def setup_inputs(seed: int=0):
    np.random.seed(seed)
    _w = jnp.asarray

    def _rec_inputs():
        import jax
        import jax.numpy as jnp
        _rk = jax.random.key(seed)
        x = jax.random.randint(jax.random.fold_in(_rk, 1), (8, 512), 0, 100, jnp.int32)
        mask_BSS_b0_1 = jnp.logical_not(jnp.ones((8, 512, 512), dtype=bool))
        fside_BSS_rel_dist = jax.random.uniform(jax.random.fold_in(_rk, 22), (8, 512, 512), jnp.float32, 0.0, 1)
        return (x, mask_BSS_b0_1, fside_BSS_rel_dist)
    x, mask_BSS_b0_1, fside_BSS_rel_dist = _rec_inputs()

    def _L0_tok_setup():
        import jax, jax.numpy as jnp
        import numpy as np
        NUM_ATOMS = 100
        DIM = 64
        LN_EPS = 1e-05
        key = jax.random.key(seed)
        ks = jax.random.split(key, 10)
        b, n, d = (4, 512, DIM)
        atom_ids = jax.random.randint(ks[0], (b, n), 0, NUM_ATOMS)
        adj_mat = jax.random.randint(ks[1], (b, n, n), 0, 2).astype(bool)
        rel_dist = jax.random.uniform(ks[2], (b, n, n), dtype=jnp.float32)
        s = 1.0 / np.sqrt(d)
        params = {'atom_embed': jax.random.normal(ks[3], (NUM_ATOMS, d), jnp.float32), 'neighbor_embed': jax.random.normal(ks[4], (NUM_ATOMS, d), jnp.float32), 'w_rd': jax.random.normal(ks[5], (d,), jnp.float32), 'w1': jax.random.normal(ks[6], (2 * d, d), jnp.float32) * s, 'b1': jnp.zeros((d,), jnp.float32), 'gamma': jnp.ones((d,), jnp.float32), 'beta': jnp.zeros((d,), jnp.float32), 'w2': jax.random.normal(ks[7], (d, d), jnp.float32) * s, 'b2': jnp.zeros((d,), jnp.float32)}
        return {'atom_ids': atom_ids, 'adj_mat': adj_mat, 'rel_dist': rel_dist, **params}
    _L0_tok_all = _L0_tok_setup()
    _L0_tok_in = {k: v for k, v in _L0_tok_all.items() if k in ('atom_embed', 'neighbor_embed', 'w_rd', 'w1', 'b1', 'gamma', 'beta', 'w2', 'b2')}
    del _L0_tok_all

    def _L0_attn_setup():
        import jax, jax.numpy as jnp
        import numpy as np
        HEAD_SIZE = 64
        HEAD_SIZE_R = HEAD_SIZE // 4
        HEAD_SIZE_C = HEAD_SIZE - HEAD_SIZE_R
        N_EMBD = 64

        def rope(x, start_pos=0):
            B, T, d = x.shape
            half = d // 2
            theta = 1.0 / 10000.0 ** (jnp.arange(half, dtype=x.dtype) / half)
            idx = jnp.arange(start_pos, start_pos + T, dtype=x.dtype)[:, None] * theta[None, :]
            sin, cos = (jnp.sin(idx), jnp.cos(idx))
            xs = x.reshape(B, T, half, 2)
            x1, x2 = (xs[..., 0], xs[..., 1])
            rot = jnp.stack([x1 * cos - x2 * sin, x1 * sin + x2 * cos], axis=-1)
            return rot.reshape(B, T, d)

        def _reference_tuple_inner(x, Wq_comp, Wkv_comp, Wqc, Wqr, Wkc, Wkr, Wv):
            c_q = x @ Wq_comp
            c_kv = x @ Wkv_comp
            q_c = c_q @ Wqc
            q_r = rope(c_q @ Wqr, start_pos=0)
            q = jnp.concatenate([q_c, q_r], axis=-1)
            k_c = c_kv @ Wkc
            k_r = rope(c_kv @ Wkr, start_pos=0)
            k = jnp.concatenate([k_c, k_r], axis=-1)
            v = c_kv @ Wv
            scale = 1.0 / jnp.sqrt(jnp.asarray(HEAD_SIZE, dtype=x.dtype))
            wei = jnp.einsum('bqd,bkd->bqk', q, k) * scale
            T_q = q.shape[1]
            mask = jnp.tril(jnp.ones((T_q, T_q), dtype=bool))
            wei = jnp.where(mask, wei, jnp.asarray(-jnp.inf, dtype=wei.dtype))
            wei = jax.nn.softmax(wei, axis=-1)
            out = jnp.einsum('bqk,bkd->bqd', wei, v)
            return (out, (k, v))
        key = jax.random.key(seed)
        ks = jax.random.split(key, 8)
        B, T = (32, 512)
        s = 0.05
        return {'x': jax.random.normal(ks[0], (B, T, N_EMBD), dtype=jnp.float32), 'Wq_comp': jax.random.normal(ks[1], (N_EMBD, N_EMBD), dtype=jnp.float32) * s, 'Wkv_comp': jax.random.normal(ks[2], (N_EMBD, N_EMBD), dtype=jnp.float32) * s, 'Wqc': jax.random.normal(ks[3], (N_EMBD, HEAD_SIZE_C), dtype=jnp.float32) * s, 'Wqr': jax.random.normal(ks[4], (N_EMBD, HEAD_SIZE_R), dtype=jnp.float32) * s, 'Wkc': jax.random.normal(ks[5], (N_EMBD, HEAD_SIZE_C), dtype=jnp.float32) * s, 'Wkr': jax.random.normal(ks[6], (N_EMBD, HEAD_SIZE_R), dtype=jnp.float32) * s, 'Wv': jax.random.normal(ks[7], (N_EMBD, HEAD_SIZE), dtype=jnp.float32) * s}
    _L0_attn_all = _L0_attn_setup()
    _L0_attn_in = {k: v for k, v in _L0_attn_all.items() if k in ('Wq_comp', 'Wkv_comp', 'Wqc', 'Wqr', 'Wkc', 'Wkr', 'Wv')}
    del _L0_attn_all

    def _L0_ffn_setup():
        import jax, jax.numpy as jnp
        import numpy as np
        DIM = 64
        HEADS = 8
        NUM_KEYS = 64
        NUM_KV = NUM_KEYS ** 2
        PK_TOPK = 16
        FINAL_TOPK = 16
        DIM_KEY = DIM // 2
        P = 2

        def _pk(x, Wq_pk, pk_keys):
            b, n, _ = x.shape
            q = (x @ Wq_pk).reshape(b, n, P, HEADS, DIM_KEY).transpose(2, 0, 1, 3, 4)
            sim = jnp.einsum('pbnhd,pkhd->pbnhk', q, pk_keys)
            scores, idx = jax.lax.top_k(sim, PK_TOPK)
            idx0 = idx[0]
            idx1 = idx[1] * NUM_KEYS
            index = (idx0[..., :, None] + idx1[..., None, :]).reshape(b, n, HEADS, PK_TOPK * PK_TOPK)
            score = (scores[0][..., :, None] + scores[1][..., None, :]).reshape(b, n, HEADS, PK_TOPK * PK_TOPK)
            final_scores, pk_idx = jax.lax.top_k(score, FINAL_TOPK)
            final_indices = jnp.take_along_axis(index, pk_idx, axis=-1)
            final_scores = jax.nn.softmax(final_scores, axis=-1)
            return (final_scores, final_indices)
        key = jax.random.key(seed)
        ks = jax.random.split(key, 7)
        b, n = (2, 256)
        std = 0.02
        x = jax.random.normal(ks[0], (b, n, DIM), dtype=jnp.float32)
        Wq_pk = jax.random.normal(ks[1], (DIM, P * HEADS * DIM_KEY), dtype=jnp.float32) * std
        pk_keys = jax.random.normal(ks[2], (P, NUM_KEYS, HEADS, DIM_KEY), dtype=jnp.float32) * std
        Wq = jax.random.normal(ks[3], (DIM, HEADS * DIM), dtype=jnp.float32) * std
        keys_table = jax.random.normal(ks[4], (NUM_KV * HEADS, DIM), dtype=jnp.float32) * std
        values_table = jax.random.normal(ks[5], (NUM_KV * HEADS, DIM), dtype=jnp.float32) * std
        Wo = jax.random.normal(ks[6], (DIM * HEADS, DIM), dtype=jnp.float32) * std
        return {'x': x, 'Wq_pk': Wq_pk, 'pk_keys': pk_keys, 'Wq': Wq, 'keys_table': keys_table, 'values_table': values_table, 'Wo': Wo}
    _L0_ffn_all = _L0_ffn_setup()
    _L0_ffn_in = {k: v for k, v in _L0_ffn_all.items() if k in ('Wq_pk', 'pk_keys', 'Wq', 'keys_table', 'values_table', 'Wo')}
    del _L0_ffn_all
    return {'x': x, 'mask_BSS_b0_1': mask_BSS_b0_1, 'fside_BSS_rel_dist': fside_BSS_rel_dist, 'L0_tok_atom_embed': _L0_tok_in['atom_embed'], 'L0_tok_neighbor_embed': _L0_tok_in['neighbor_embed'], 'L0_tok_w_rd': _L0_tok_in['w_rd'], 'L0_tok_w1': _L0_tok_in['w1'], 'L0_tok_b1': _L0_tok_in['b1'], 'L0_tok_gamma': _L0_tok_in['gamma'], 'L0_tok_beta': _L0_tok_in['beta'], 'L0_tok_w2': _L0_tok_in['w2'], 'L0_tok_b2': _L0_tok_in['b2'], 'L0_attn_Wq_comp': _L0_attn_in['Wq_comp'], 'L0_attn_Wkv_comp': _L0_attn_in['Wkv_comp'], 'L0_attn_Wqc': _L0_attn_in['Wqc'], 'L0_attn_Wqr': _L0_attn_in['Wqr'], 'L0_attn_Wkc': _L0_attn_in['Wkc'], 'L0_attn_Wkr': _L0_attn_in['Wkr'], 'L0_attn_Wv': _L0_attn_in['Wv'], 'L0_ffn_Wq_pk': _L0_ffn_in['Wq_pk'], 'L0_ffn_pk_keys': _L0_ffn_in['pk_keys'], 'L0_ffn_Wq': _L0_ffn_in['Wq'], 'L0_ffn_keys_table': _L0_ffn_in['keys_table'], 'L0_ffn_values_table': _L0_ffn_in['values_table'], 'L0_ffn_Wo': _L0_ffn_in['Wo']}

def reference(x, mask_BSS_b0_1, fside_BSS_rel_dist, L0_tok_atom_embed, L0_tok_neighbor_embed, L0_tok_w_rd, L0_tok_w1, L0_tok_b1, L0_tok_gamma, L0_tok_beta, L0_tok_w2, L0_tok_b2, L0_attn_Wq_comp, L0_attn_Wkv_comp, L0_attn_Wqc, L0_attn_Wqr, L0_attn_Wkc, L0_attn_Wkr, L0_attn_Wv, L0_ffn_Wq_pk, L0_ffn_pk_keys, L0_ffn_Wq, L0_ffn_keys_table, L0_ffn_values_table, L0_ffn_Wo):
    import jax
    import jax.numpy as jnp

    def _L0_tok_ref(atom_ids, adj_mat, rel_dist, atom_embed, neighbor_embed, w_rd, w1, b1, gamma, beta, w2, b2):
        import jax, jax.numpy as jnp
        import numpy as np
        NUM_ATOMS = 100
        DIM = 64
        LN_EPS = 1e-05
        n = atom_ids.shape[-1]
        eye = jnp.eye(n, dtype=bool)
        mask = adj_mat & ~eye
        embeds = atom_embed[atom_ids]
        nbr_embeds = neighbor_embed[atom_ids]
        weighted = jnp.where(mask, rel_dist, jnp.zeros((), rel_dist.dtype))
        neighbor_feats = jnp.einsum('bij,bjd->bid', weighted, nbr_embeds) * w_rd
        x = jnp.concatenate([embeds, neighbor_feats], axis=-1)
        h = x @ w1 + b1
        mu = jnp.mean(h, axis=-1, keepdims=True)
        var = jnp.mean(jnp.square(h - mu), axis=-1, keepdims=True)
        h = (h - mu) * jax.lax.rsqrt(var + LN_EPS) * gamma + beta
        h = jax.nn.silu(h)
        return h @ w2 + b2

    def _L0_attn_ref(x, Wq_comp, Wkv_comp, Wqc, Wqr, Wkc, Wkr, Wv):
        import jax, jax.numpy as jnp
        import numpy as np
        HEAD_SIZE = 64
        HEAD_SIZE_R = HEAD_SIZE // 4
        HEAD_SIZE_C = HEAD_SIZE - HEAD_SIZE_R
        N_EMBD = 64

        def rope(x, start_pos=0):
            B, T, d = x.shape
            half = d // 2
            theta = 1.0 / 10000.0 ** (jnp.arange(half, dtype=x.dtype) / half)
            idx = jnp.arange(start_pos, start_pos + T, dtype=x.dtype)[:, None] * theta[None, :]
            sin, cos = (jnp.sin(idx), jnp.cos(idx))
            xs = x.reshape(B, T, half, 2)
            x1, x2 = (xs[..., 0], xs[..., 1])
            rot = jnp.stack([x1 * cos - x2 * sin, x1 * sin + x2 * cos], axis=-1)
            return rot.reshape(B, T, d)

        def _reference_tuple_inner(x, Wq_comp, Wkv_comp, Wqc, Wqr, Wkc, Wkr, Wv):
            c_q = x @ Wq_comp
            c_kv = x @ Wkv_comp
            q_c = c_q @ Wqc
            q_r = rope(c_q @ Wqr, start_pos=0)
            q = jnp.concatenate([q_c, q_r], axis=-1)
            k_c = c_kv @ Wkc
            k_r = rope(c_kv @ Wkr, start_pos=0)
            k = jnp.concatenate([k_c, k_r], axis=-1)
            v = c_kv @ Wv
            scale = 1.0 / jnp.sqrt(jnp.asarray(HEAD_SIZE, dtype=x.dtype))
            wei = jnp.einsum('bqd,bkd->bqk', q, k) * scale
            T_q = q.shape[1]
            mask = jnp.tril(jnp.ones((T_q, T_q), dtype=bool))
            wei = jnp.where(mask, wei, jnp.asarray(-jnp.inf, dtype=wei.dtype))
            wei = jax.nn.softmax(wei, axis=-1)
            out = jnp.einsum('bqk,bkd->bqd', wei, v)
            return (out, (k, v))
        return _reference_tuple_inner(x, Wq_comp, Wkv_comp, Wqc, Wqr, Wkc, Wkr, Wv)[0]

    def _L0_ffn_ref(x, Wq_pk, pk_keys, Wq, keys_table, values_table, Wo):
        import jax, jax.numpy as jnp
        import numpy as np
        DIM = 64
        HEADS = 8
        NUM_KEYS = 64
        NUM_KV = NUM_KEYS ** 2
        PK_TOPK = 16
        FINAL_TOPK = 16
        DIM_KEY = DIM // 2
        P = 2

        def _pk(x, Wq_pk, pk_keys):
            b, n, _ = x.shape
            q = (x @ Wq_pk).reshape(b, n, P, HEADS, DIM_KEY).transpose(2, 0, 1, 3, 4)
            sim = jnp.einsum('pbnhd,pkhd->pbnhk', q, pk_keys)
            scores, idx = jax.lax.top_k(sim, PK_TOPK)
            idx0 = idx[0]
            idx1 = idx[1] * NUM_KEYS
            index = (idx0[..., :, None] + idx1[..., None, :]).reshape(b, n, HEADS, PK_TOPK * PK_TOPK)
            score = (scores[0][..., :, None] + scores[1][..., None, :]).reshape(b, n, HEADS, PK_TOPK * PK_TOPK)
            final_scores, pk_idx = jax.lax.top_k(score, FINAL_TOPK)
            final_indices = jnp.take_along_axis(index, pk_idx, axis=-1)
            final_scores = jax.nn.softmax(final_scores, axis=-1)
            return (final_scores, final_indices)
        b, n, d = x.shape
        q = (x @ Wq).reshape(b, n, HEADS, DIM) * DIM ** (-0.5)
        kv_scores, indices = _pk(x, Wq_pk, pk_keys)
        offsets = jnp.arange(HEADS, dtype=indices.dtype) * NUM_KV
        ind = indices + offsets[None, None, :, None]
        k = jnp.einsum('bnhk,bnhkd->bnhd', kv_scores, keys_table[ind])
        v = jnp.einsum('bnhk,bnhkd->bnhd', kv_scores, values_table[ind])
        sim = jnp.einsum('bihd,bjhd->bhij', q, k)
        neg = -jnp.finfo(sim.dtype).max
        causal = jnp.tril(jnp.ones((n, n), dtype=bool))
        sim = jnp.where(causal, sim, neg)
        attn = jax.nn.softmax(sim, axis=-1)
        out = jnp.einsum('bhij,bjhd->bhid', attn, v)
        out = out.transpose(0, 2, 1, 3).reshape(b, n, HEADS * DIM)
        return out @ Wo
    h = _L0_tok_ref(x, mask_BSS_b0_1, fside_BSS_rel_dist, L0_tok_atom_embed, L0_tok_neighbor_embed, L0_tok_w_rd, L0_tok_w1, L0_tok_b1, L0_tok_gamma, L0_tok_beta, L0_tok_w2, L0_tok_b2)
    h = h + _L0_attn_ref(_layernorm(h, axis=-1), L0_attn_Wq_comp, L0_attn_Wkv_comp, L0_attn_Wqc, L0_attn_Wqr, L0_attn_Wkc, L0_attn_Wkr, L0_attn_Wv)
    h = h + _L0_ffn_ref(_layernorm(h, axis=-1), L0_ffn_Wq_pk, L0_ffn_pk_keys, L0_ffn_Wq, L0_ffn_keys_table, L0_ffn_values_table, L0_ffn_Wo)
    return h

_drawn_inputs = setup_inputs


def setup_inputs(seed=0):
    import zlib

    import numpy as np

    out = dict(_drawn_inputs(seed))
    spreads = {'L0_tok_b1': (0.0, 0.1),
     'L0_tok_gamma': (1.0, 0.2),
     'L0_tok_beta': (0.0, 0.1),
     'L0_tok_b2': (0.0, 0.1)}
    factors = {'L0_attn_Wq_comp': 8.0,
     'L0_attn_Wqc': 8.0,
     'L0_attn_Wqr': 8.0,
     'L0_attn_Wkc': 8.0,
     'L0_attn_Wkr': 8.0,
     'L0_ffn_Wq_pk': 8.0,
     'L0_ffn_pk_keys': 8.0,
     'L0_ffn_Wq': 64.0,
     'L0_ffn_keys_table': 64.0,
     'L0_ffn_values_table': 8.0,
     'L0_ffn_Wo': 8.0}
    for name, (base, spread) in spreads.items():
        noise = np.random.default_rng([zlib.crc32(name.encode()), seed]).standard_normal(out[name].shape)
        drawn = base * np.exp(spread * noise) if base else spread * noise
        out[name] = jnp.asarray(drawn.astype(out[name].dtype))
    for name, factor in factors.items():
        out[name] = (out[name] * factor).astype(out[name].dtype)
    return out
```

```python
import concourse.bass as bass
from concourse import mybir
from contextlib import ExitStack

F32 = mybir.dt.float32
U32 = mybir.dt.uint32
U8 = mybir.dt.uint8
ALU = mybir.AluOpType
ACT = mybir.ActivationFunctionType
AX = mybir.AxisListType

P = 128
NB, T, D = 8, 512, 64
NT = T // P
H = 8
NK = 64
TOPK = 16
LANES = 2 * H
SLOTS = 8
EPS = 1e-5
LOW = -3.0e38

STAIR = [(0, 1, 16), (1, 1, 8), (2, 2, 5), (4, 4, 3), (8, 8, 1)]
NC = sum(na * nb for _, na, nb in STAIR)


class Phase:

    def __init__(self, plan, full, free, banks):
        self.uses, self.at = {}, {}
        self.full_sem, self.free_sem, self.banks = full, free, banks
        for step, bank in plan:
            self.at[step] = (bank, self.uses.get(bank, 0))
            self.uses[bank] = self.uses.get(bank, 0) + 1

    def bank(self, step):
        return self.banks[self.at[step][0]]

    def full(self, step):
        return self.full_sem[self.at[step][0]]

    def free(self, step):
        return self.free_sem[self.at[step][0]]

    def wait_full(self, eng, b, step):
        bank, n = self.at[step]
        eng.wait_ge(self.full_sem[bank], b * self.uses[bank] + n + 1)

    def wait_free(self, eng, b, step):
        bank, n = self.at[step]
        eng.wait_ge(self.free_sem[bank], b * self.uses[bank] + n + 1)

    def wait_room(self, eng, b, step):
        bank, n = self.at[step]
        if n:
            eng.wait_ge(self.free_sem[bank], b * self.uses[bank] + n)

    def wait_all_free(self, eng, b):
        for bank, k in self.uses.items():
            eng.wait_ge(self.free_sem[bank], b * k + k)


def attention_plan(heads, projected):
    plan = []
    for h in range(heads):
        if projected:
            plan += [(f"k{h}", "M0"), (f"q{h}", "M1")]
        plan += [(f"S{h},{i}", f"S{i % 2}") for i in range(NT)]
        plan += [(f"P{h},{i}", f"T{i % 2}") for i in range(NT)]
        plan += [(f"o{h}", "O0")]
    return plan


FRONT = ([(f"rel{j}", f"T{j % 2}") for j in range(NT)]
         + [("nbr", "M0"), ("emb", "T0"), ("h", "M1"), ("silu", "T1"), ("tok", "M0"), ("ln1", "T0"),
            ("comp", "M1"), ("qA", "M0"), ("qB", "O0"), ("kA", "O1"), ("kB", "M1"), ("v", "T1")]
         + attention_plan(1, False) + [("att", "M0"), ("ln2", "T0")]
         + [(f"qpk{m}", f"M{(m + 1) % 2}") for m in range(4)]
         + [(f"sim{t},{s}", f"O{s}") for t in range(NT) for s in range(2)])
BACK = attention_plan(H, True) + [("out", "M0")]


def tower(nc, d, out):
    ctx = ExitStack()
    with ctx:
        def sb(name, shape, dt=F32):
            return ctx.enter_context(nc.sbuf_tensor(name, shape, dt))

        def sem(name):
            return ctx.enter_context(nc.semaphore(name))

        CONST = ["ident", "noteye", "causal", "iota", "head_base", "w1", "b1", "gamma", "beta", "b2"]
        K64 = ["cosq", "sinq", "cosk", "sink", "w2", "wcomp", "wq", "wpk", "wo"]
        HIGH = ["wrd", "wk_a", "wk_b", "wv"]
        w = {n: sb(n, list(d[n].shape)) for n in CONST + K64 + ["wq_a", "wq_b", "keys"]}
        for n in HIGH:
            w[n] = sb(n, [P, d[n].shape[1]])
        ids = sb("ids", [P, NT], U32)
        rel = sb("rel", [P, NT, T])
        adj = sb("adj", [P, NT, T], U8)
        emb = sb("emb", [P, NT, 2 * D])
        wide = sb("wide", [P, NT, T])
        relT = wide[:, :, :]
        qpkT = wide[:, :, :]
        probT = wide[:, :, :]
        xT = sb("xT", [P, T])
        compT = xT[:, :]
        hid = sb("hid", [P, NT, D])
        sq = sb("sq", [P, NT, D])
        gate = sb("gate", [P, NT, D])
        stat = sb("stat", [P, 4, NT])
        tok = sb("tok", [P, NT, D])
        lnT = sb("lnT", [D, T])
        actT = lnT[:, :]
        qT = sb("qT", [D, T])
        kT = sb("kT", [D, T])
        val = sb("val", [P, NT, D])
        sim = sb("sim", [P, NT, LANES * NK])
        prob = [sb(f"prob{i}", [P, T]) for i in range(2)]
        ropeA, ropeB = prob[0][0:D, :], prob[1][0:D, :]
        negmax = sb("negmax", [P, 2])
        psum = sb("psum", [P, 2])
        pinv = sb("pinv", [P, 2])
        oT = sb("oT", [D, H, T])
        best = sb("best", [P, LANES, TOPK])
        besti = sb("besti", [P, LANES, TOPK], U32)
        bestf = sb("bestf", [P, LANES, TOPK])
        cand = sb("cand", [P, H, NC])
        candi = sb("candi", [P, H, NC])
        fin = sb("fin", [P, H, TOPK])
        finp = sb("finp", [P, H, TOPK], U32)
        finf = sb("finf", [P, H, TOPK])
        hot = sb("hot", [P, 2 * TOPK, NC])
        fsum = sb("fsum", [P, 2, H])
        idx = sb("idx", [P, NT, H * TOPK], U32)
        wgt = sb("wgt", [P, NT, H * TOPK])
        rows = sb("rows", [P, SLOTS, TOPK, 2 * D])
        kv = sb("kv", [P, NT, H, 2 * D])
        lnT_cur = sb("lnT_cur", [D, T])
        tok_cur = sb("tok_cur", [P, NT, D])
        khT = [sb(f"khT{i}", [D, T]) for i in range(2)]
        qhT = [sb(f"qhT{i}", [D, T]) for i in range(2)]
        y = sb("y", [P, NT, D])

        names = ["T0", "T1", "M0", "M1", "S0", "S1", "O0", "O1"]
        banks = {n: ctx.enter_context(nc.psum_tensor(n, [P, 512], F32)) for n in names}
        front = Phase(FRONT, {n: sem("front_full_" + n) for n in names},
                      {n: sem("front_free_" + n) for n in names}, banks)
        back = Phase(BACK, {n: sem("back_full_" + n) for n in names},
                     {n: sem("back_free_" + n) for n in names}, banks)

        weights_in, rel_in, adj_in, ids_in = sem("weights_in"), sem("rel_in"), sem("adj_in"), sem("ids_in")
        emb_in = sem("emb_in")
        rel_masked = sem("rel_masked")
        var_ready, rstd_ready, log_done = sem("var_ready"), sem("rstd_ready"), sem("log_done")
        gate_in, gate_exp = sem("gate_in"), sem("gate_exp")
        silu_ready = sem("silu_ready")
        ln_ready = sem("ln_ready")
        qk_ready = sem("qk_ready")
        front_max, front_norm = sem("front_max"), sem("front_norm")
        back_max, back_norm = sem("back_max"), sem("back_norm")
        fin_ready, fin_exp = sem("fin_ready"), sem("fin_exp")
        idx_ready = sem("idx_ready")
        slot_free = sem("slot_free")
        rows_in = [sem(f"rows_in{i}") for i in range(SLOTS)]
        cur_ready = sem("cur_ready")
        y_out = sem("y_out")
        pe_holds, pool_holds, dve_holds = sem("pe_holds"), sem("pool_holds"), sem("dve_holds")
        vec = sem("vec")

        NW = 16 * len(w)
        TILES = NT * H
        block = ctx.enter_context(nc.Block())

        def hold(eng, own):
            eng.sem_inc(own, 1)

        @block.sync
        def _(sp):
            for n in w:
                dst = w[n][:, :] if n not in HIGH else w[n][D:P, :]
                sp.dma_start(dst, d[n]).then_inc(weights_in, 16)

            def load(b):
                if not isinstance(b, int):
                    front.wait_full(sp, b - 1, "rel3")
                    sp.wait_ge(emb_in, (b - 1) * 64 + 64)
                one = bass.ds(b, 1)
                sp.dma_start(ids[:, :], d["x"][one, :, :].rearrange("b p t -> p (b t)")).then_inc(ids_in, 16)
                sp.dma_start(adj[:, :, :], d["adj"][one, :, :].rearrange("b (t p) j -> p (b t) j", p=P)).then_inc(adj_in, 16)
                sp.dma_start(rel[:, :, :], d["rel"][one, :, :].rearrange("b (t p) j -> p (b t) j", p=P)).then_inc(rel_in, 16)

            def store(b):
                back.wait_free(sp, b, "out")
                one = bass.ds(b, 1)
                sp.dma_start(out[one, :, :].rearrange("b (t p) n -> p (b t) n", p=P), y[:, :, :]).then_inc(y_out, 16)

            sp.sem_inc(y_out, 16)
            load(0)
            with sp.Fori(0, NB - 1) as c:
                load(c + 1)
                store(c)
            store(NB - 1)
            sp.wait_ge(y_out, 16 * NB + 16)

        @block.gpsimd
        def _(pool):
            def gather_embeddings(b):
                pool.wait_ge(ids_in, b * 16 + 16)
                if not isinstance(b, int):
                    front.wait_full(pool, b - 1, "nbr")
                    front.wait_full(pool, b - 1, "emb")
                hold(pool, pool_holds)
                for t in range(NT):
                    pool.indirect_dma_start(emb[:, t, :], None, d["embed"], bass.IndirectOffsetOnAxis(ids[:, t:t + 1], 0)).then_inc(emb_in, 16)

            def gather_rows(c):
                for t in range(NT):
                    pool.wait_ge(idx_ready, c * NT + t + 1)
                    for h in range(H):
                        g = t * H + h
                        pool.wait_ge(slot_free, c * TILES + g + 1)
                        hold(pool, pool_holds)
                        for s in range(TOPK):
                            pool.indirect_dma_start(rows[:, g % SLOTS, s, :], None, d["table"],
                                                    bass.IndirectOffsetOnAxis(idx[:, t, h * TOPK + s:h * TOPK + s + 1], 0)).then_inc(rows_in[g % SLOTS], 16)

            gather_embeddings(0)
            with pool.Fori(0, NB - 1) as c:
                gather_embeddings(c + 1)
                gather_rows(c)
            gather_rows(NB - 1)

        @block.tensor
        def _(pe):
            mm = nc.tensor.matmul

            def transposes(ph, b, step, parts, width):
                ph.wait_room(pe, b, step)
                if width < P:
                    hold(pe, pe_holds)
                for t, a in enumerate(parts):
                    last = nc.tensor.transpose(ph.bank(step)[0:width, t * P:(t + 1) * P], a, w["ident"][:, :])
                last.then_inc(ph.full(step), 1)

            def attend(ph, b, heads, before, queries, keys, values, norm):
                order = [(h, i) for h in range(heads) for i in range(NT)]

                def scores(h, i):
                    if i == 0:
                        before(h)
                    step = f"S{h},{i}"
                    ph.wait_room(pe, b, step)
                    n = (i + 1) * P
                    mm(ph.bank(step)[:, 0:n], queries(h)[:, i * P:(i + 1) * P], keys(h)[:, 0:n],
                       start=True, stop=True).then_inc(ph.full(step), 1)

                scores(0, 0)
                for n, (h, i) in enumerate(order):
                    if n + 1 < len(order):
                        scores(*order[n + 1])
                    pe.wait_ge(norm, b * len(order) + n + 1)
                    transposes(ph, b, f"P{h},{i}", [prob[i % 2][:, k * P:(k + 1) * P] for k in range(i + 1)], P)
                    if i == NT - 1:
                        ph.wait_free(pe, b, f"P{h},{i - 1}")
                        ph.wait_free(pe, b, f"P{h},{i}")
                        ph.wait_room(pe, b, f"o{h}")
                        for k in range(NT):
                            last = mm(ph.bank(f"o{h}")[0:D, k * P:], values(h, k), probT[:, k, k * P:],
                                      start=(k == 0), stop=(k == NT - 1))
                        last.then_inc(ph.full(f"o{h}"), 1)

            def run_front(b):
                pe.wait_ge(rel_masked, b + 1)
                for j in range(NT):
                    transposes(front, b, f"rel{j}", [rel[:, t, j * P:(j + 1) * P] for t in range(NT)], P)
                pe.wait_ge(emb_in, b * 64 + 64)
                transposes(front, b, "emb", [emb[:, t, :] for t in range(NT)], P)
                front.wait_free(pe, b, "rel3")
                front.wait_free(pe, b, "rel2")
                for j in range(NT):
                    last = mm(front.bank("nbr")[:, :], emb[:, j, :], relT[:, j, :], start=(j == 0), stop=(j == NT - 1))
                last.then_inc(front.full("nbr"), 1)
                front.wait_free(pe, b, "emb")
                front.wait_free(pe, b, "nbr")
                for t in range(NT):
                    last = mm(front.bank("h")[:, t * D:(t + 1) * D], xT[:, t * P:(t + 1) * P], w["w1"][:, :], start=True, stop=True)
                last.then_inc(front.full("h"), 1)
                pe.wait_ge(silu_ready, b + 1)
                transposes(front, b, "silu", [hid[:, t, :] for t in range(NT)], D)
                front.wait_free(pe, b, "silu")
                front.wait_room(pe, b, "tok")
                for t in range(NT):
                    last = mm(front.bank("tok")[:, t * D:(t + 1) * D], actT[:, t * P:(t + 1) * P], w["w2"][:, :], start=True, stop=True)
                last.then_inc(front.full("tok"), 1)
                pe.wait_ge(ln_ready, b * 2 + 1)
                transposes(front, b, "ln1", [hid[:, t, :] for t in range(NT)], D)
                front.wait_free(pe, b, "ln1")
                front.wait_room(pe, b, "comp")
                mm(front.bank("comp")[:, :], w["wcomp"][:, :], lnT[:, :], start=True, stop=True).then_inc(front.full("comp"), 1)
                front.wait_free(pe, b, "comp")
                for step, lhs, lo in (("qA", "wq_a", 0), ("qB", "wq_b", 0), ("kA", "wk_a", D), ("kB", "wk_b", D)):
                    front.wait_room(pe, b, step)
                    hold(pe, pe_holds)
                    mm(front.bank(step)[0:D, :], w[lhs][lo:lo + D, :], compT[lo:lo + D, :], start=True, stop=True).then_inc(front.full(step), 1)
                front.wait_room(pe, b, "v")
                hold(pe, pe_holds)
                for t in range(NT):
                    last = mm(front.bank("v")[:, t * D:(t + 1) * D], compT[D:P, t * P:(t + 1) * P], w["wv"][D:P, :], start=True, stop=True)
                last.then_inc(front.full("v"), 1)
                pe.wait_ge(qk_ready, b + 1)
                front.wait_free(pe, b, "v")
                attend(front, b, 1, lambda h: None, lambda h: qT, lambda h: kT, lambda h, k: val[:, k, :], front_norm)
                front.wait_free(pe, b, "o0")
                front.wait_room(pe, b, "att")
                for t in range(NT):
                    last = mm(front.bank("att")[:, t * D:(t + 1) * D], oT[:, 0, t * P:(t + 1) * P], w["ident"][0:D, 0:D], start=True, stop=True)
                last.then_inc(front.full("att"), 1)
                pe.wait_ge(ln_ready, b * 2 + 2)
                transposes(front, b, "ln2", [hid[:, t, :] for t in range(NT)], D)
                front.wait_free(pe, b, "ln2")
                for m in range(4):
                    front.wait_room(pe, b, f"qpk{m}")
                    mm(front.bank(f"qpk{m}")[:, :], w["wpk"][:, m * P:(m + 1) * P], lnT[:, :], start=True, stop=True).then_inc(front.full(f"qpk{m}"), 1)
                front.wait_free(pe, b, "qpk2")
                front.wait_free(pe, b, "qpk3")
                for t in range(NT):
                    for s in range(2):
                        front.wait_room(pe, b, f"sim{t},{s}")
                        for g in range(2):
                            m = 2 * s + g
                            last = mm(front.bank(f"sim{t},{s}")[:, g * 256:(g + 1) * 256], qpkT[:, m, t * P:(t + 1) * P],
                                      w["keys"][:, m * 256:(m + 1) * 256], start=True, stop=True)
                        last.then_inc(front.full(f"sim{t},{s}"), 1)
                front.wait_all_free(pe, b)

            def run_back(c):
                pe.wait_ge(cur_ready, c + 1)
                pe.wait_ge(slot_free, c * TILES + TILES + SLOTS)

                def before(h):
                    transposes(back, c, f"k{h}", [kv[:, t, h, :] for t in range(NT)], P)
                    back.wait_room(pe, c, f"q{h}")
                    hold(pe, pe_holds)
                    mm(back.bank(f"q{h}")[0:D, :], w["wq"][:, h * D:(h + 1) * D], lnT_cur[:, :], start=True, stop=True).then_inc(back.full(f"q{h}"), 1)
                    back.wait_free(pe, c, f"k{h}")
                    back.wait_free(pe, c, f"q{h}")

                attend(back, c, H, before, lambda h: qhT[h % 2], lambda h: khT[h % 2], lambda h, k: kv[:, k, h, D:2 * D], back_norm)
                back.wait_free(pe, c, f"o{H - 1}")
                back.wait_room(pe, c, "out")
                for t in range(NT):
                    for h in range(H):
                        last = mm(back.bank("out")[:, t * D:(t + 1) * D], oT[:, h, t * P:(t + 1) * P], w["wo"][:, h * D:(h + 1) * D],
                                  start=(h == 0), stop=(h == H - 1))
                last.then_inc(back.full("out"), 1)
                back.wait_all_free(pe, c)

            pe.wait_ge(weights_in, NW)
            run_front(0)
            with pe.Fori(0, NB - 1) as c:
                run_front(c + 1)
                run_back(c)
            run_back(NB - 1)

        @block.scalar
        def _(act):
            fn = nc.scalar.activation

            def copy(ph, b, step, dst, src, scale=1.0):
                ph.wait_full(act, b, step)
                fn(dst, src, ACT.Copy, scale=scale).then_inc(ph.free(step), 1)

            def rstd(b, n):
                act.wait_ge(var_ready, b * 3 + n + 1)
                fn(stat[:, 2, :], stat[:, 1, :], ACT.Ln).then_inc(log_done, 1)
                act.wait_ge(log_done, b * 3 + n + 1)
                fn(stat[:, 3, :], stat[:, 2, :], ACT.Exp, scale=-0.5).then_inc(rstd_ready, 1)

            def attend(ph, b, heads, before, norm_max):
                order = [(h, i) for h in range(heads) for i in range(NT)]

                def exps(n):
                    h, i = order[n]
                    if i == 0:
                        before(h)
                    if n >= 2:
                        ph.wait_full(act, b, "P%d,%d" % order[n - 2])
                    act.wait_ge(norm_max, b * len(order) + n + 1)
                    m = (i + 1) * P
                    fn(prob[i % 2][:, 0:m], ph.bank(f"S{h},{i}")[:, 0:m], ACT.Exp, bias=negmax[:, i % 2:i % 2 + 1],
                       accum_out=psum[:, i % 2:i % 2 + 1]).then_inc(ph.free(f"S{h},{i}"), 1)

                exps(0)
                for n, (h, i) in enumerate(order):
                    if n + 1 < len(order):
                        exps(n + 1)
                    step = f"P{h},{i}"
                    if i == 0 and h:
                        ph.wait_full(act, b, f"o{h - 1}")
                    copy(ph, b, step, probT[:, 0:i + 1, i * P:(i + 1) * P],
                         ph.bank(step)[:, 0:(i + 1) * P].rearrange("p (k q) -> p k q", q=P))
                    if i == NT - 1:
                        copy(ph, b, f"o{h}", oT[:, h, :], ph.bank(f"o{h}")[0:D, :])

            def run_front(b):
                for j in range(NT):
                    copy(front, b, f"rel{j}", relT[:, j, :], front.bank(f"rel{j}")[:, :])
                copy(front, b, "emb", xT[0:D, :], front.bank("emb")[0:D, :])
                copy(front, b, "nbr", xT[D:P, :], front.bank("nbr")[D:P, :], scale=w["wrd"][D:P, 0:1])
                rstd(b, 0)
                act.wait_ge(gate_in, b + 1)
                fn(gate[:, :, :], hid[:, :, :], ACT.Exp, scale=-1.0).then_inc(gate_exp, 1)
                copy(front, b, "silu", actT[:, :], front.bank("silu")[0:D, :])
                rstd(b, 1)
                copy(front, b, "ln1", lnT[:, :], front.bank("ln1")[0:D, :])
                copy(front, b, "comp", compT[:, :], front.bank("comp")[:, :])
                copy(front, b, "v", val[:, :, :], front.bank("v")[:, 0:NT * D].rearrange("p (t n) -> p t n", n=D))
                attend(front, b, 1, lambda h: None, front_max)
                rstd(b, 2)
                copy(front, b, "ln2", lnT[:, :], front.bank("ln2")[0:D, :])
                for m in range(4):
                    copy(front, b, f"qpk{m}", qpkT[:, m, :], front.bank(f"qpk{m}")[:, :])
                for t in range(NT):
                    if not isinstance(b, int):
                        act.wait_ge(fin_ready, b * NT)
                    for s in range(2):
                        copy(front, b, f"sim{t},{s}", sim[:, t, s * 512:(s + 1) * 512], front.bank(f"sim{t},{s}")[:, :])

            def fin_exps(b, t):
                act.wait_ge(fin_ready, b * NT + t + 1)
                fn(fin[:, :, :], fin[:, :, :], ACT.Exp).then_inc(fin_exp, 1)

            def keep(c):
                front.wait_free(act, c, "ln2")
                fn(lnT_cur[:, :], lnT[:, :], ACT.Copy).then_inc(cur_ready, 1)

            def run_back(c):
                def before(h):
                    copy(back, c, f"k{h}", khT[h % 2][:, :], back.bank(f"k{h}")[0:D, :])
                    copy(back, c, f"q{h}", qhT[h % 2][:, :], back.bank(f"q{h}")[0:D, :], scale=D ** -0.5)

                attend(back, c, H, before, back_max)

            act.wait_ge(weights_in, NW)
            run_front(0)
            for t in range(NT):
                fin_exps(0, t)
            with act.Fori(0, NB - 1) as c:
                keep(c)
                act.wait_ge(cur_ready, c + 1)
                run_front(c + 1)
                for t in range(NT):
                    fin_exps(c + 1, t)
                run_back(c)
            keep(NB - 1)
            run_back(NB - 1)

        @block.vector
        def _(dve):
            V = nc.vector
            steps = [0]

            def mark(ins):
                steps[0] += 1
                ins.then_inc(vec, 1)
                return steps[0]

            def wait(n):
                dve.wait_ge(vec, n)

            def done(ins):
                wait(mark(ins))

            def section_end():
                wait(steps[0])
                hold(dve, dve_holds)
                dve.sem_clear(vec)
                steps[0] = 0

            def over(a, n):
                return a.unsqueeze(len(a.shape)).to_broadcast(list(a.shape) + [n])

            def tiles(a):
                return a.unsqueeze(1).to_broadcast([P, NT, D])

            def grid(step):
                return front.bank(step)[:, 0:NT * D].rearrange("p (t n) -> p t n", n=D)

            def normalise(b, n, src, dst):
                done(V.tensor_reduce(stat[:, 0, :], src, AX.X, ALU.add))
                done(V.tensor_scalar(stat[:, 0, :], stat[:, 0, :], 1.0 / D, None, ALU.mult))
                done(V.tensor_tensor(dst, src, over(stat[:, 0, :], D), ALU.subtract))
                done(V.tensor_tensor(sq[:, :, :], dst, dst, ALU.mult))
                done(V.tensor_reduce(stat[:, 1, :], sq[:, :, :], AX.X, ALU.add))
                V.tensor_scalar(stat[:, 1, :], stat[:, 1, :], 1.0 / D, EPS, ALU.mult, ALU.add).then_inc(var_ready, 1)
                dve.wait_ge(rstd_ready, b * 3 + n + 1)

            def attend(ph, b, heads, norm_max, norm):
                order = [(h, i) for h in range(heads) for i in range(NT)]

                def maxima(n):
                    h, i = order[n]
                    step = f"S{h},{i}"
                    S = ph.bank(step)
                    ph.wait_full(dve, b, step)
                    done(V.tensor_tensor(S[:, i * P:(i + 1) * P], S[:, i * P:(i + 1) * P], w["causal"][:, :], ALU.add))
                    if n >= 2:
                        ph.wait_free(dve, b, "S%d,%d" % order[n - 2])
                    V.tensor_reduce(negmax[:, i % 2:i % 2 + 1], S[:, 0:(i + 1) * P], AX.X, ALU.max, negate=True).then_inc(norm_max, 1)

                maxima(0)
                for n, (h, i) in enumerate(order):
                    if n + 1 < len(order):
                        maxima(n + 1)
                    ph.wait_free(dve, b, f"S{h},{i}")
                    j = i % 2
                    done(V.reciprocal(pinv[:, j:j + 1], psum[:, j:j + 1]))
                    m = (i + 1) * P
                    V.tensor_scalar(prob[j][:, 0:m], prob[j][:, 0:m], pinv[:, j:j + 1], None, ALU.mult).then_inc(norm, 1)

            def run_front(b):
                dve.wait_ge(rel_in, b * 16 + 16)
                dve.wait_ge(adj_in, b * 16 + 16)
                for t in range(NT):
                    own = rel[:, t, t * P:(t + 1) * P]
                    n = mark(V.tensor_tensor(own, own, w["noteye"][:, :], ALU.mult))
                wait(n)
                for t in range(NT):
                    last = V.tensor_tensor(rel[:, t, :], rel[:, t, :], adj[:, t, :], ALU.mult)
                last.then_inc(rel_masked, 1)
                front.wait_full(dve, b, "h")
                if not isinstance(b, int):
                    front.wait_full(dve, b - 1, "ln2")
                V.tensor_tensor(gate[:, :, :], grid("h"), tiles(w["b1"][:, :]), ALU.add).then_inc(front.free("h"), 1)
                front.wait_free(dve, b, "h")
                normalise(b, 0, gate[:, :, :], hid[:, :, :])
                done(V.tensor_tensor(hid[:, :, :], hid[:, :, :], over(stat[:, 3, :], D), ALU.mult))
                done(V.tensor_tensor(hid[:, :, :], hid[:, :, :], tiles(w["gamma"][:, :]), ALU.mult))
                V.tensor_tensor(hid[:, :, :], hid[:, :, :], tiles(w["beta"][:, :]), ALU.add).then_inc(gate_in, 1)
                dve.wait_ge(gate_exp, b + 1)
                done(V.tensor_scalar(gate[:, :, :], gate[:, :, :], 1.0, None, ALU.add))
                done(V.reciprocal(gate[:, :, :], gate[:, :, :]))
                V.tensor_tensor(hid[:, :, :], hid[:, :, :], gate[:, :, :], ALU.mult).then_inc(silu_ready, 1)
                front.wait_full(dve, b, "tok")
                V.tensor_tensor(tok[:, :, :], grid("tok"), tiles(w["b2"][:, :]), ALU.add).then_inc(front.free("tok"), 1)
                front.wait_free(dve, b, "tok")
                front.wait_full(dve, b, "silu")
                normalise(b, 1, tok[:, :, :], hid[:, :, :])
                V.tensor_tensor(hid[:, :, :], hid[:, :, :], over(stat[:, 3, :], D), ALU.mult).then_inc(ln_ready, 1)
                for dst, a, s, cos, sin in ((qT, "qA", "qB", "cosq", "sinq"), (kT, "kA", "kB", "cosk", "sink")):
                    front.wait_full(dve, b, a)
                    V.tensor_tensor(ropeA[:, :], front.bank(a)[0:D, :], w[cos][:, :], ALU.mult).then_inc(front.free(a), 1)
                    front.wait_full(dve, b, s)
                    V.tensor_tensor(ropeB[:, :], front.bank(s)[0:D, :], w[sin][:, :], ALU.mult).then_inc(front.free(s), 1)
                    front.wait_free(dve, b, a)
                    front.wait_free(dve, b, s)
                    if dst is qT:
                        done(V.tensor_tensor(dst[:, :], ropeA[:, :], ropeB[:, :], ALU.add))
                    else:
                        V.tensor_tensor(dst[:, :], ropeA[:, :], ropeB[:, :], ALU.add).then_inc(qk_ready, 1)
                attend(front, b, 1, front_max, front_norm)
                front.wait_full(dve, b, "att")
                V.tensor_tensor(tok[:, :, :], grid("att"), tok[:, :, :], ALU.add).then_inc(front.free("att"), 1)
                front.wait_free(dve, b, "att")
                front.wait_full(dve, b, "ln1")
                normalise(b, 2, tok[:, :, :], hid[:, :, :])
                V.tensor_tensor(hid[:, :, :], hid[:, :, :], over(stat[:, 3, :], D), ALU.mult).then_inc(ln_ready, 1)
                section_end()

            def top(b, t):
                front.wait_free(dve, b, f"sim{t},0")
                front.wait_free(dve, b, f"sim{t},1")
                done(V.tensor_copy(fsum[:, 0, :], sim[:, t, 0:H]))

                def top16(lanes, src, vals, inds):
                    m = [mark(V.max(vals(r)[:, 0:8], src(r))) for r in range(lanes)]
                    for r in range(lanes):
                        wait(m[r])
                        n = mark(V.max_index(inds(r)[:, 0:8], vals(r)[:, 0:8], src(r)))
                        m[r] = n
                    for r in range(lanes):
                        wait(m[r])
                        m[r] = mark(V.match_replace(src(r), vals(r)[:, 0:8], src(r), LOW))
                    for r in range(lanes):
                        wait(m[r])
                        m[r] = mark(V.max(vals(r)[:, 8:16], src(r)))
                    for r in range(lanes):
                        wait(m[r])
                        m[r] = mark(V.max_index(inds(r)[:, 8:16], vals(r)[:, 8:16], src(r)))
                    wait(m[-1])

                top16(LANES, lambda r: sim[:, t, r * NK:(r + 1) * NK], lambda r: best[:, r, :], lambda r: besti[:, r, :])
                mark(V.tensor_copy(bestf[:, 0:H, :], besti[:, 0:H, :]))
                done(V.tensor_scalar(bestf[:, H:LANES, :], besti[:, H:LANES, :], float(NK), None, ALU.mult))
                at = 0
                for a, na, nb in STAIR:
                    for src, dst in ((best, cand), (bestf, candi)):
                        n = mark(V.tensor_tensor(
                            dst[:, :, at:at + na * nb].rearrange("p h (a b) -> p h a b", b=nb),
                            src[:, 0:H, a:a + na].unsqueeze(3).to_broadcast([P, H, na, nb]),
                            src[:, H:LANES, 0:nb].unsqueeze(2).to_broadcast([P, H, na, nb]), ALU.add))
                    at += na * nb
                wait(n)
                top16(H, lambda h: cand[:, h, :], lambda h: fin[:, h, :], lambda h: finp[:, h, :])
                mark(V.tensor_copy(finf[:, :, :], finp[:, :, :]))
                done(V.tensor_copy(fsum[:, 0, :], fin[:, :, 0]))
                V.tensor_tensor(fin[:, :, :], fin[:, :, :], over(fsum[:, 0, :], TOPK), ALU.subtract).then_inc(fin_ready, 1)
                for h in range(0, H, 2):
                    lane = hot[:, :, :].rearrange("p (h s) n -> p h s n", h=2)
                    done(V.tensor_tensor(hot[:, :, :], over(finf[:, h:h + 2, :].rearrange("p h s -> p (h s)"), NC),
                                         w["iota"][:, :].unsqueeze(1).to_broadcast([P, 2 * TOPK, NC]), ALU.is_equal))
                    done(V.tensor_tensor(lane, lane, candi[:, h:h + 2, :].unsqueeze(2).to_broadcast([P, 2, TOPK, NC]), ALU.mult))
                    done(V.tensor_reduce(bestf[:, h:h + 2, :].rearrange("p h s -> p (h s)"), hot[:, :, :], AX.X, ALU.add))
                V.tensor_tensor(idx[:, t, :], bestf[:, 0:H, :].rearrange("p h s -> p (h s)"), w["head_base"][:, :], ALU.add).then_inc(idx_ready, 1)
                dve.wait_ge(fin_exp, b * NT + t + 1)
                done(V.tensor_reduce(fsum[:, 0, :], fin[:, :, :], AX.X, ALU.add))
                done(V.reciprocal(fsum[:, 1, :], fsum[:, 0, :]))
                done(V.tensor_tensor(wgt[:, t, :].rearrange("p (h s) -> p h s", h=H), fin[:, :, :], over(fsum[:, 1, :], TOPK), ALU.mult))
                section_end()

            def combine(c, t):
                marks = {}

                def scale(h):
                    g = t * H + h
                    slot = rows[:, g % SLOTS, :, :]
                    dve.wait_ge(rows_in[g % SLOTS], (c * (TILES // SLOTS) + g // SLOTS + 1) * 16 * TOPK)
                    marks[h] = mark(V.tensor_tensor(slot, slot, over(wgt[:, t, h * TOPK:(h + 1) * TOPK], 2 * D), ALU.mult))

                scale(0)
                for h in range(H):
                    if h + 1 < H:
                        scale(h + 1)
                    wait(marks[h])
                    V.tensor_reduce(kv[:, t, h, :], rows[:, (t * H + h) % SLOTS, :, :].rearrange("p s n -> p n s"), AX.X, ALU.add).then_inc(slot_free, 1)
                section_end()

            def keep(c):
                mark(V.tensor_copy(tok_cur[:, :, :], tok[:, :, :]))
                section_end()

            def run_back(c):
                attend(back, c, H, back_max, back_norm)
                back.wait_full(dve, c, "out")
                dve.wait_ge(y_out, c * 16 + 16)
                V.tensor_tensor(y[:, :, :], back.bank("out")[:, 0:NT * D].rearrange("p (t n) -> p t n", n=D), tok_cur[:, :, :], ALU.add).then_inc(back.free("out"), 1)
                back.wait_free(dve, c, "out")
                section_end()

            V.memset(y[:, :, :], 0.0).then_inc(slot_free, SLOTS)
            dve.wait_ge(weights_in, NW)
            run_front(0)
            for t in range(NT):
                top(0, t)
            with dve.Fori(0, NB - 1) as c:
                keep(c)
                run_front(c + 1)
                for t in range(NT):
                    combine(c, t)
                    top(c + 1, t)
                run_back(c)
            keep(NB - 1)
            for t in range(NT):
                combine(NB - 1, t)
            run_back(NB - 1)


def kernel(**inputs):
    import numpy as np
    import concourse.bacc as bacc
    from concourse.bass_utils import run_bass_kernel_spmd as run

    f = np.float32
    a = {k: np.asarray(v) for k, v in inputs.items()}

    def rep(v):
        return np.ascontiguousarray(np.broadcast_to(v.reshape(1, -1), (P, v.size)))

    n_rope = D // 4
    rot = np.arange(n_rope) ^ 1
    half = n_rope // 2
    theta = (f(1.0) / (f(10000.0) ** (np.arange(half, dtype=f) / f(half)))).astype(f)
    angle = np.arange(T, dtype=f)[:, None] * theta[None, :]
    cos, sin = np.ones((D, T), f), np.zeros((D, T), f)
    cos[D - n_rope:] = np.repeat(np.cos(angle).T, 2, axis=0)
    sin[D - n_rope:] = np.repeat(np.sin(angle).T, 2, axis=0)
    sin[D - n_rope::2] *= f(-1.0)
    scale = f(D ** -0.5)
    pk = a["L0_ffn_pk_keys"]
    keys = np.zeros((4, P, 4, NK), f)
    for s in range(2):
        for h in range(H):
            keys[2 * s + h // 4, (h % 4) * 32:(h % 4 + 1) * 32, h % 4, :] = pk[s, :, h, :].T
    d = {
        "x": a["x"].view(np.uint32).reshape(NB, NT, P).transpose(0, 2, 1), "adj": a["mask_BSS_b0_1"], "rel": a["fside_BSS_rel_dist"],
        "embed": np.concatenate([a["L0_tok_atom_embed"], a["L0_tok_neighbor_embed"]], axis=1),
        "table": np.concatenate([a["L0_ffn_keys_table"], a["L0_ffn_values_table"]], axis=1),
        "ident": np.eye(P, dtype=f), "noteye": (1 - np.eye(P)).astype(f),
        "causal": np.triu(np.full((P, P), LOW, f), 1),
        "iota": rep(np.arange(NC, dtype=f)), "head_base": rep(np.repeat(np.arange(H, dtype=f) * NK * NK, TOPK)),
        "cosq": cos * scale, "sinq": sin * scale, "cosk": cos, "sink": sin,
        "wrd": a["L0_tok_w_rd"].reshape(D, 1), "w1": a["L0_tok_w1"], "b1": rep(a["L0_tok_b1"]),
        "gamma": rep(a["L0_tok_gamma"]), "beta": rep(a["L0_tok_beta"]), "w2": a["L0_tok_w2"], "b2": rep(a["L0_tok_b2"]),
        "wcomp": np.concatenate([a["L0_attn_Wq_comp"], a["L0_attn_Wkv_comp"]], axis=1),
        "wq_a": np.concatenate([a["L0_attn_Wqc"], a["L0_attn_Wqr"]], axis=1),
        "wq_b": np.concatenate([a["L0_attn_Wqc"], a["L0_attn_Wqr"][:, rot]], axis=1),
        "wk_a": np.concatenate([a["L0_attn_Wkc"], a["L0_attn_Wkr"]], axis=1),
        "wk_b": np.concatenate([a["L0_attn_Wkc"], a["L0_attn_Wkr"][:, rot]], axis=1),
        "wv": a["L0_attn_Wv"], "wpk": a["L0_ffn_Wq_pk"], "wq": a["L0_ffn_Wq"],
        "keys": keys.transpose(1, 0, 2, 3).reshape(P, 4 * 4 * NK),
        "wo": a["L0_ffn_Wo"].reshape(H, D, D).transpose(1, 0, 2).reshape(D, H * D),
    }
    d = {k: np.ascontiguousarray(v) for k, v in d.items()}
    nc = bacc.Bacc("TRN2", target_bir_lowering=False, num_devices=1)
    aps = {k: nc.dram_tensor("in_" + k, v.shape, mybir.dt.from_np(v.dtype), kind="ExternalInput").ap() for k, v in d.items()}
    out = nc.dram_tensor("out", (NB, T, D), F32, kind="ExternalOutput").ap()
    tower(nc, aps, out)
    r = run(nc, [{"in_" + k: v for k, v in d.items()}], core_ids=[0])
    return r.results[0]["out"]
```

```python
import concourse.bass as bass
from concourse import mybir
from contextlib import ExitStack

F32 = mybir.dt.float32
U32 = mybir.dt.uint32
U8 = mybir.dt.uint8
ALU = mybir.AluOpType
ACT = mybir.ActivationFunctionType
AX = mybir.AxisListType

P = 128
NB, T, D = 8, 512, 64
NT = T // P
H = 8
NK = 64
TOPK = 16
LANES = 2 * H
SLOTS = 8
EPS = 1e-5
LOW = -3.0e38

STAIR = [(0, 1, 16), (1, 1, 8), (2, 2, 5), (4, 4, 3), (8, 8, 1)]
PACE_LAST = 3
PACE = [2, 2, 2, 3]
NC = sum(na * nb for _, na, nb in STAIR)


class Phase:

    def __init__(self, plan, full, free, banks):
        self.uses, self.at = {}, {}
        self.full_sem, self.free_sem, self.banks = full, free, banks
        for step, bank in plan:
            self.at[step] = (bank, self.uses.get(bank, 0))
            self.uses[bank] = self.uses.get(bank, 0) + 1

    def bank(self, step):
        return self.banks[self.at[step][0]]

    def full(self, step):
        return self.full_sem[self.at[step][0]]

    def free(self, step):
        return self.free_sem[self.at[step][0]]

    def wait_full(self, eng, b, step):
        bank, n = self.at[step]
        eng.wait_ge(self.full_sem[bank], b * self.uses[bank] + n + 1)

    def wait_free(self, eng, b, step):
        bank, n = self.at[step]
        eng.wait_ge(self.free_sem[bank], b * self.uses[bank] + n + 1)

    def wait_room(self, eng, b, step):
        bank, n = self.at[step]
        if n:
            eng.wait_ge(self.free_sem[bank], b * self.uses[bank] + n)

    def wait_all_free(self, eng, b):
        for bank, k in self.uses.items():
            eng.wait_ge(self.free_sem[bank], b * k + k)


def attention_plan(heads, projected):
    plan = []
    for h in range(heads):
        if projected:
            plan += [(f"k{h}", "M0"), (f"q{h}", "M1")]
        plan += [(f"S{h},{i}", f"S{i % 2}") for i in range(NT)]
        plan += [(f"P{h},{i}", f"T{i % 2}") for i in range(NT)]
        plan += [(f"o{h}", "O0")]
    return plan


FRONT = ([(f"rel{j}", f"T{j % 2}") for j in range(NT)]
         + [("nbr", "M0"), ("emb", "T0"), ("h", "M1"), ("silu", "T1"), ("tok", "M0"), ("ln1", "T0"),
            ("comp", "M1"), ("qA", "M0"), ("qB", "O0"), ("kA", "O1"), ("kB", "M1"), ("v", "T1")]
         + attention_plan(1, False) + [("att", "M0"), ("ln2", "T0")]
         + [(f"qpk{m}", f"M{(m + 1) % 2}") for m in range(4)]
         + [(f"sim{t},{s}", f"O{s}") for t in range(NT) for s in range(2)])
BACK = attention_plan(H, True) + [("out", "M0")]


def tower(nc, d, out):
    ctx = ExitStack()
    with ctx:
        def sb(name, shape, dt=F32):
            return ctx.enter_context(nc.sbuf_tensor(name, shape, dt))

        def sem(name):
            return ctx.enter_context(nc.semaphore(name))

        CONST = ["ident", "noteye", "causal", "iota", "head_base", "w1", "b1", "gamma", "beta", "b2"]
        K64 = ["cosq", "sinq", "cosk", "sink", "w2", "wcomp", "wq", "wpk", "wo"]
        HIGH = ["wrd", "wk_a", "wk_b", "wv"]
        w = {n: sb(n, list(d[n].shape)) for n in CONST + K64 + ["wq_a", "wq_b", "keys"]}
        for n in HIGH:
            w[n] = sb(n, [P, d[n].shape[1]])
        ids = sb("ids", [P, NT], U32)
        rel = sb("rel", [P, NT, T])
        adj = sb("adj", [P, NT, T], U8)
        emb = sb("emb", [P, NT, 2 * D])
        wide = sb("wide", [P, NT, T])
        relT = wide[:, :, :]
        qpkT = wide[:, :, :]
        probT = wide[:, :, :]
        xT = sb("xT", [P, T])
        compT = xT[:, :]
        hid = sb("hid", [P, NT, D])
        sq = sb("sq", [P, NT, D])
        gate = sb("gate", [P, NT, D])
        stat = sb("stat", [P, 4, NT])
        tok = sb("tok", [P, NT, D])
        lnT = sb("lnT", [D, T])
        actT = lnT[:, :]
        qT = sb("qT", [D, T])
        kT = sb("kT", [D, T])
        val = sb("val", [P, NT, D])
        sim = sb("sim", [P, NT, LANES * NK])
        prob = [sb(f"prob{i}", [P, T]) for i in range(2)]
        ropeA, ropeB = prob[0][0:D, :], prob[1][0:D, :]
        negmax = sb("negmax", [P, 2])
        psum = sb("psum", [P, 2])
        pinv = sb("pinv", [P, 2])
        oT = sim[0:D, :, :].rearrange("p t (a n) -> p (t a) n", n=T)
        best = sb("best", [P, LANES, TOPK])
        besti = sb("besti", [P, LANES, TOPK], U32)
        bestf = sb("bestf", [P, LANES, TOPK])
        cand = sb("cand", [P, H, NC])
        candi = sb("candi", [P, H, NC])
        fin = sb("fin", [P, H, TOPK])
        finp = sb("finp", [P, H, TOPK], U32)
        finf = sb("finf", [P, H, TOPK])
        hot = sb("hot", [P, 2 * TOPK, NC])
        fsum = sb("fsum", [P, 2, H])
        idx = sb("idx", [P, NT, H * TOPK], U32)
        wgt = sb("wgt", [P, NT, H * TOPK])
        rows = sb("rows", [P, SLOTS, TOPK, 2 * D])
        kv = sb("kv", [P, NT, H, 2 * D])
        kv_cur = sb("kv_cur", [P, NT, H, 2 * D])
        lnT_cur = sb("lnT_cur", [D, T])
        tok_cur = sb("tok_cur", [P, NT, D])
        khT = [sb(f"khT{i}", [D, T]) for i in range(2)]
        qhT = [sb(f"qhT{i}", [D, T]) for i in range(2)]
        y = sb("y", [P, NT, D])

        names = ["T0", "T1", "M0", "M1", "S0", "S1", "O0", "O1"]
        banks = {n: ctx.enter_context(nc.psum_tensor(n, [P, 512], F32)) for n in names}
        front = Phase(FRONT, {n: sem("front_full_" + n) for n in names},
                      {n: sem("front_free_" + n) for n in names}, banks)
        back = Phase(BACK, {n: sem("back_full_" + n) for n in names},
                     {n: sem("back_free_" + n) for n in names}, banks)

        weights_in, rel_in, adj_in, ids_in = sem("weights_in"), sem("rel_in"), sem("adj_in"), sem("ids_in")
        emb_in = sem("emb_in")
        rel_masked = sem("rel_masked")
        var_ready, rstd_ready, log_done = sem("var_ready"), sem("rstd_ready"), sem("log_done")
        gate_in, gate_exp = sem("gate_in"), sem("gate_exp")
        silu_ready = sem("silu_ready")
        ln_ready = sem("ln_ready")
        qk_ready = sem("qk_ready")
        front_max, front_norm = sem("front_max"), sem("front_norm")
        back_max, back_norm = sem("back_max"), sem("back_norm")
        fin_ready, fin_exp = sem("fin_ready"), sem("fin_exp")
        idx_ready = sem("idx_ready")
        slot_free = sem("slot_free")
        rows_in = [sem(f"rows_in{i}") for i in range(SLOTS)]
        cur_ready = sem("cur_ready")
        kv_ready = sem("kv_ready")
        y_out = sem("y_out")
        pe_holds, pool_holds, dve_holds = sem("pe_holds"), sem("pool_holds"), sem("dve_holds")
        vec = sem("vec")

        NW = 16 * len(w)
        TILES = NT * H
        block = ctx.enter_context(nc.Block())

        order = ["ident", "noteye"] + [n for n in w if n not in ("ident", "noteye")]

        def load_weights(eng, names):
            for n in names:
                dst = w[n][:, :] if n not in HIGH else w[n][D:P, :]
                eng.dma_start(dst, d[n]).then_inc(weights_in, 16)

        def place(c, g):
            return (g % NT, g // NT) if is_last(c) else divmod(g, H)

        def is_last(c):
            return isinstance(c, int) and c == NB - 1

        def is_first(b):
            return isinstance(b, int) and b == 0

        def hold(eng, own):
            eng.sem_inc(own, 1)

        @block.sync
        def _(sp):
            def load(b):
                if not is_first(b):
                    front.wait_full(sp, b - 1, "rel3")
                    sp.wait_ge(emb_in, (b - 1) * 64 + 64)
                one = bass.ds(b, 1)
                sp.dma_start(ids[:, :], d["x"][one, :, :].rearrange("b p t -> p (b t)")).then_inc(ids_in, 16)
                sp.dma_start(adj[:, :, :], d["adj"][one, :, :].rearrange("b (t p) j -> p (b t) j", p=P)).then_inc(adj_in, 16)
                sp.dma_start(rel[:, :, :], d["rel"][one, :, :].rearrange("b (t p) j -> p (b t) j", p=P)).then_inc(rel_in, 16)

            def store(b):
                back.wait_free(sp, b, "out")
                one = bass.ds(b, 1)
                sp.dma_start(out[one, :, :].rearrange("b (t p) n -> p (b t) n", p=P), y[:, :, :]).then_inc(y_out, 16)

            sp.sem_inc(y_out, 16)
            load(0)
            load_weights(sp, order[0::2])
            load(1)
            with sp.Fori(1, NB - 1) as c:
                load(c + 1)
                store(c - 1)
            store(NB - 2)
            store(NB - 1)
            sp.wait_ge(y_out, 16 * NB + 16)

        @block.gpsimd
        def _(pool):
            def gather_embeddings(b):
                pool.wait_ge(ids_in, b * 16 + 16)
                if not is_first(b):
                    front.wait_full(pool, b - 1, "nbr")
                    front.wait_full(pool, b - 1, "emb")
                hold(pool, pool_holds)
                for t in range(NT):
                    pool.indirect_dma_start(emb[:, t, :], None, d["embed"], bass.IndirectOffsetOnAxis(ids[:, t:t + 1], 0)).then_inc(emb_in, 16)

            def gather_rows(c):
                for g in range(TILES):
                    t, h = place(c, g)
                    if h % 2 == 0:
                        pool.wait_ge(idx_ready, (c * NT + t) * (H // 2) + h // 2 + 1)
                    pool.wait_ge(slot_free, c * TILES + g + 1)
                    hold(pool, pool_holds)
                    for s in range(TOPK):
                        pool.indirect_dma_start(rows[:, g % SLOTS, s, :], None, d["table"],
                                                bass.IndirectOffsetOnAxis(idx[:, t, h * TOPK + s:h * TOPK + s + 1], 0)).then_inc(rows_in[g % SLOTS], 16)

            gather_embeddings(0)
            with pool.Fori(0, NB - 1) as c:
                gather_embeddings(c + 1)
                gather_rows(c)
            gather_rows(NB - 1)

        @block.tensor
        def _(pe):
            mm = nc.tensor.matmul

            def transposes(ph, b, step, parts, width):
                ph.wait_room(pe, b, step)
                if width < P:
                    hold(pe, pe_holds)
                for t, a in enumerate(parts):
                    last = nc.tensor.transpose(ph.bank(step)[0:width, t * P:(t + 1) * P], a, w["ident"][:, :])
                last.then_inc(ph.full(step), 1)

            def attend(ph, b, heads, before, queries, keys, values, norm):
                order = [(h, i) for h in range(heads) for i in range(NT)]

                def scores(h, i):
                    if i == 0:
                        before(h)
                    step = f"S{h},{i}"
                    ph.wait_room(pe, b, step)
                    n = (i + 1) * P
                    mm(ph.bank(step)[:, 0:n], queries(h)[:, i * P:(i + 1) * P], keys(h)[:, 0:n],
                       start=True, stop=True).then_inc(ph.full(step), 1)

                scores(0, 0)
                for n, (h, i) in enumerate(order):
                    if n + 1 < len(order):
                        scores(*order[n + 1])
                    pe.wait_ge(norm, b * len(order) + n + 1)
                    transposes(ph, b, f"P{h},{i}", [prob[i % 2][:, k * P:(k + 1) * P] for k in range(i + 1)], P)
                    if i == NT - 1:
                        ph.wait_free(pe, b, f"P{h},{i - 1}")
                        ph.wait_free(pe, b, f"P{h},{i}")
                        ph.wait_room(pe, b, f"o{h}")
                        for k in range(NT):
                            last = mm(ph.bank(f"o{h}")[0:D, k * P:], values(h, k), probT[:, k, k * P:],
                                      start=(k == 0), stop=(k == NT - 1))
                        last.then_inc(ph.full(f"o{h}"), 1)

            def run_front(b):
                pe.wait_ge(rel_masked, b + 1)
                for j in range(NT):
                    transposes(front, b, f"rel{j}", [rel[:, t, j * P:(j + 1) * P] for t in range(NT)], P)
                pe.wait_ge(emb_in, b * 64 + 64)
                transposes(front, b, "emb", [emb[:, t, :] for t in range(NT)], P)
                front.wait_free(pe, b, "rel3")
                front.wait_free(pe, b, "rel2")
                for j in range(NT):
                    last = mm(front.bank("nbr")[:, :], emb[:, j, :], relT[:, j, :], start=(j == 0), stop=(j == NT - 1))
                last.then_inc(front.full("nbr"), 1)
                front.wait_free(pe, b, "emb")
                front.wait_free(pe, b, "nbr")
                for t in range(NT):
                    last = mm(front.bank("h")[:, t * D:(t + 1) * D], xT[:, t * P:(t + 1) * P], w["w1"][:, :], start=True, stop=True)
                last.then_inc(front.full("h"), 1)
                pe.wait_ge(silu_ready, b + 1)
                transposes(front, b, "silu", [hid[:, t, :] for t in range(NT)], D)
                front.wait_free(pe, b, "silu")
                front.wait_room(pe, b, "tok")
                for t in range(NT):
                    last = mm(front.bank("tok")[:, t * D:(t + 1) * D], actT[:, t * P:(t + 1) * P], w["w2"][:, :], start=True, stop=True)
                last.then_inc(front.full("tok"), 1)
                pe.wait_ge(ln_ready, b * 2 + 1)
                transposes(front, b, "ln1", [hid[:, t, :] for t in range(NT)], D)
                front.wait_free(pe, b, "ln1")
                front.wait_room(pe, b, "comp")
                mm(front.bank("comp")[:, :], w["wcomp"][:, :], lnT[:, :], start=True, stop=True).then_inc(front.full("comp"), 1)
                front.wait_free(pe, b, "comp")
                for step, lhs, lo in (("qA", "wq_a", 0), ("qB", "wq_b", 0), ("kA", "wk_a", D), ("kB", "wk_b", D)):
                    front.wait_room(pe, b, step)
                    hold(pe, pe_holds)
                    mm(front.bank(step)[0:D, :], w[lhs][lo:lo + D, :], compT[lo:lo + D, :], start=True, stop=True).then_inc(front.full(step), 1)
                front.wait_room(pe, b, "v")
                hold(pe, pe_holds)
                for t in range(NT):
                    last = mm(front.bank("v")[:, t * D:(t + 1) * D], compT[D:P, t * P:(t + 1) * P], w["wv"][D:P, :], start=True, stop=True)
                last.then_inc(front.full("v"), 1)
                pe.wait_ge(qk_ready, b + 1)
                front.wait_free(pe, b, "v")
                attend(front, b, 1, lambda h: None, lambda h: qT, lambda h: kT, lambda h, k: val[:, k, :], front_norm)
                front.wait_free(pe, b, "o0")
                front.wait_room(pe, b, "att")
                for t in range(NT):
                    last = mm(front.bank("att")[:, t * D:(t + 1) * D], oT[:, 0, t * P:(t + 1) * P], w["ident"][0:D, 0:D], start=True, stop=True)
                last.then_inc(front.full("att"), 1)
                pe.wait_ge(ln_ready, b * 2 + 2)
                transposes(front, b, "ln2", [hid[:, t, :] for t in range(NT)], D)
                front.wait_free(pe, b, "ln2")
                for m in range(4):
                    front.wait_room(pe, b, f"qpk{m}")
                    mm(front.bank(f"qpk{m}")[:, :], w["wpk"][:, m * P:(m + 1) * P], lnT[:, :], start=True, stop=True).then_inc(front.full(f"qpk{m}"), 1)
                front.wait_free(pe, b, "qpk2")
                front.wait_free(pe, b, "qpk3")
                for t in range(NT):
                    for s in range(2):
                        front.wait_room(pe, b, f"sim{t},{s}")
                        for g in range(2):
                            m = 2 * s + g
                            last = mm(front.bank(f"sim{t},{s}")[:, g * 256:(g + 1) * 256], qpkT[:, m, t * P:(t + 1) * P],
                                      w["keys"][:, m * 256:(m + 1) * 256], start=True, stop=True)
                        last.then_inc(front.full(f"sim{t},{s}"), 1)
                front.wait_all_free(pe, b)

            def run_back(c):
                src = kv if is_last(c) else kv_cur
                pe.wait_ge(cur_ready, c + 1)
                if not is_last(c):
                    pe.wait_ge(kv_ready, c + 1)

                def before(h):
                    if is_last(c):
                        pe.wait_ge(slot_free, c * TILES + (h + 1) * NT + SLOTS)
                    transposes(back, c, f"k{h}", [src[:, t, h, :] for t in range(NT)], P)
                    back.wait_room(pe, c, f"q{h}")
                    hold(pe, pe_holds)
                    mm(back.bank(f"q{h}")[0:D, :], w["wq"][:, h * D:(h + 1) * D], lnT_cur[:, :], start=True, stop=True).then_inc(back.full(f"q{h}"), 1)
                    back.wait_free(pe, c, f"k{h}")
                    back.wait_free(pe, c, f"q{h}")

                attend(back, c, H, before, lambda h: qhT[h % 2], lambda h: khT[h % 2], lambda h, k: src[:, k, h, D:2 * D], back_norm)
                back.wait_free(pe, c, f"o{H - 1}")
                back.wait_room(pe, c, "out")
                for t in range(NT):
                    for h in range(H):
                        last = mm(back.bank("out")[:, t * D:(t + 1) * D], oT[:, h, t * P:(t + 1) * P], w["wo"][:, h * D:(h + 1) * D],
                                  start=(h == 0), stop=(h == H - 1))
                last.then_inc(back.full("out"), 1)
                back.wait_all_free(pe, c)

            pe.wait_ge(weights_in, NW)
            run_front(0)
            run_front(1)
            with pe.Fori(1, NB - 1) as c:
                run_back(c - 1)
                run_front(c + 1)
            run_back(NB - 2)
            run_back(NB - 1)

        @block.scalar
        def _(act):
            fn = nc.scalar.activation

            def copy(ph, b, step, dst, src, scale=1.0):
                ph.wait_full(act, b, step)
                fn(dst, src, ACT.Copy, scale=scale).then_inc(ph.free(step), 1)

            def rstd(b, n):
                act.wait_ge(var_ready, b * 3 + n + 1)
                fn(stat[:, 2, :], stat[:, 1, :], ACT.Ln).then_inc(log_done, 1)
                act.wait_ge(log_done, b * 3 + n + 1)
                fn(stat[:, 3, :], stat[:, 2, :], ACT.Exp, scale=-0.5).then_inc(rstd_ready, 1)

            def attend(ph, b, heads, before, norm_max, scored):
                order = [(h, i) for h in range(heads) for i in range(NT)]

                def exps(n):
                    h, i = order[n]
                    if i == 0:
                        before(h)
                    if n >= 2:
                        ph.wait_full(act, b, "P%d,%d" % order[n - 2])
                    act.wait_ge(norm_max, b * len(order) + n + 1)
                    m = (i + 1) * P
                    fn(prob[i % 2][:, 0:m], ph.bank(f"S{h},{i}")[:, 0:m], ACT.Exp, bias=negmax[:, i % 2:i % 2 + 1],
                       accum_out=psum[:, i % 2:i % 2 + 1]).then_inc(ph.free(f"S{h},{i}"), 1)

                exps(0)
                for n, (h, i) in enumerate(order):
                    if n + 1 < len(order):
                        exps(n + 1)
                    step = f"P{h},{i}"
                    if i == 0 and h:
                        ph.wait_full(act, b, f"o{h - 1}")
                    copy(ph, b, step, probT[:, 0:i + 1, i * P:(i + 1) * P],
                         ph.bank(step)[:, 0:(i + 1) * P].rearrange("p (k q) -> p k q", q=P))
                    if i == NT - 1:
                        if h == 0 and scored is not None:
                            act.wait_ge(idx_ready, scored)
                        copy(ph, b, f"o{h}", oT[:, h, :], ph.bank(f"o{h}")[0:D, :])

            def run_front(b):
                for j in range(NT):
                    copy(front, b, f"rel{j}", relT[:, j, :], front.bank(f"rel{j}")[:, :])
                copy(front, b, "emb", xT[0:D, :], front.bank("emb")[0:D, :])
                copy(front, b, "nbr", xT[D:P, :], front.bank("nbr")[D:P, :], scale=w["wrd"][D:P, 0:1])
                rstd(b, 0)
                act.wait_ge(gate_in, b + 1)
                fn(gate[:, :, :], hid[:, :, :], ACT.Exp, scale=-1.0).then_inc(gate_exp, 1)
                copy(front, b, "silu", actT[:, :], front.bank("silu")[0:D, :])
                rstd(b, 1)
                copy(front, b, "ln1", lnT[:, :], front.bank("ln1")[0:D, :])
                copy(front, b, "comp", compT[:, :], front.bank("comp")[:, :])
                copy(front, b, "v", val[:, :, :], front.bank("v")[:, 0:NT * D].rearrange("p (t n) -> p t n", n=D))
                attend(front, b, 1, lambda h: None, front_max, None if is_first(b) else b * NT * (H // 2))
                rstd(b, 2)
                copy(front, b, "ln2", lnT[:, :], front.bank("ln2")[0:D, :])
                for m in range(4):
                    copy(front, b, f"qpk{m}", qpkT[:, m, :], front.bank(f"qpk{m}")[:, :])
                for t in range(NT):
                    for s in range(2):
                        copy(front, b, f"sim{t},{s}", sim[:, t, s * 512:(s + 1) * 512], front.bank(f"sim{t},{s}")[:, :])

            def fin_exps(b, t):
                act.wait_ge(fin_ready, b * NT + t + 1)
                fn(fin[:, :, :], fin[:, :, :], ACT.Exp).then_inc(fin_exp, 1)

            def keep(c):
                front.wait_free(act, c, "ln2")
                fn(lnT_cur[:, :], lnT[:, :], ACT.Copy).then_inc(cur_ready, 1)

            def run_back(c):
                def before(h):
                    copy(back, c, f"k{h}", khT[h % 2][:, :], back.bank(f"k{h}")[0:D, :])
                    copy(back, c, f"q{h}", qhT[h % 2][:, :], back.bank(f"q{h}")[0:D, :], scale=D ** -0.5)

                attend(back, c, H, before, back_max, (c + 1 if is_last(c) else c + 2) * NT * (H // 2))

            def keep_kv(c):
                act.wait_ge(slot_free, c * TILES + TILES + SLOTS)
                if not is_first(c):
                    back.wait_full(act, c - 1, "out")
                fn(kv_cur[:, :, :, :], kv[:, :, :, :], ACT.Copy).then_inc(kv_ready, 1)

            load_weights(act, order[1::2])
            act.wait_ge(weights_in, NW)
            def prepare_next(c):
                keep(c)
                act.wait_ge(cur_ready, c + 1)
                run_front(c + 1)
                for t in range(NT):
                    fin_exps(c + 1, t)

            run_front(0)
            for t in range(NT):
                fin_exps(0, t)
            prepare_next(0)
            with act.Fori(1, NB - 1) as c:
                keep_kv(c - 1)
                run_back(c - 1)
                prepare_next(c)
            keep_kv(NB - 2)
            run_back(NB - 2)
            keep(NB - 1)
            run_back(NB - 1)

        @block.vector
        def _(dve):
            V = nc.vector
            steps = [0]

            def mark(ins):
                steps[0] += 1
                ins.then_inc(vec, 1)
                return steps[0]

            def wait(n):
                dve.wait_ge(vec, n)

            def done(ins):
                wait(mark(ins))

            def section_end():
                wait(steps[0])
                hold(dve, dve_holds)
                dve.sem_clear(vec)
                steps[0] = 0

            def over(a, n):
                return a.unsqueeze(len(a.shape)).to_broadcast(list(a.shape) + [n])

            def tiles(a):
                return a.unsqueeze(1).to_broadcast([P, NT, D])

            def grid(step):
                return front.bank(step)[:, 0:NT * D].rearrange("p (t n) -> p t n", n=D)

            def normalise(b, n, src, dst):
                done(V.tensor_reduce(stat[:, 0, :], src, AX.X, ALU.add))
                done(V.tensor_scalar(stat[:, 0, :], stat[:, 0, :], 1.0 / D, None, ALU.mult))
                done(V.tensor_tensor(dst, src, over(stat[:, 0, :], D), ALU.subtract))
                done(V.tensor_tensor(sq[:, :, :], dst, dst, ALU.mult))
                done(V.tensor_reduce(stat[:, 1, :], sq[:, :, :], AX.X, ALU.add))
                V.tensor_scalar(stat[:, 1, :], stat[:, 1, :], 1.0 / D, EPS, ALU.mult, ALU.add).then_inc(var_ready, 1)
                dve.wait_ge(rstd_ready, b * 3 + n + 1)

            def attend(ph, b, heads, norm_max, norm, sums=lambda h: 0):
                order = [(h, i) for h in range(heads) for i in range(NT)]

                def maxima(n):
                    h, i = order[n]
                    step = f"S{h},{i}"
                    S = ph.bank(step)
                    ph.wait_full(dve, b, step)
                    done(V.tensor_tensor(S[:, i * P:(i + 1) * P], S[:, i * P:(i + 1) * P], w["causal"][:, :], ALU.add))
                    if n >= 2:
                        ph.wait_free(dve, b, "S%d,%d" % order[n - 2])
                    V.tensor_reduce(negmax[:, i % 2:i % 2 + 1], S[:, 0:(i + 1) * P], AX.X, ALU.max, negate=True).then_inc(norm_max, 1)

                maxima(0)
                for n, (h, i) in enumerate(order):
                    yield sums(min(n + 1, len(order) - 1) // NT)
                    if n + 1 < len(order):
                        maxima(n + 1)
                    ph.wait_free(dve, b, f"S{h},{i}")
                    j = i % 2
                    done(V.reciprocal(pinv[:, j:j + 1], psum[:, j:j + 1]))
                    m = (i + 1) * P
                    V.tensor_scalar(prob[j][:, 0:m], prob[j][:, 0:m], pinv[:, j:j + 1], None, ALU.mult).then_inc(norm, 1)

            def run_front(b):
                dve.wait_ge(rel_in, b * 16 + 16)
                dve.wait_ge(adj_in, b * 16 + 16)
                for t in range(NT):
                    own = rel[:, t, t * P:(t + 1) * P]
                    n = mark(V.tensor_tensor(own, own, w["noteye"][:, :], ALU.mult))
                wait(n)
                for t in range(NT):
                    last = V.tensor_tensor(rel[:, t, :], rel[:, t, :], adj[:, t, :], ALU.mult)
                last.then_inc(rel_masked, 1)
                yield 0
                front.wait_full(dve, b, "h")
                if not is_first(b):
                    front.wait_full(dve, b - 1, "ln2")
                V.tensor_tensor(gate[:, :, :], grid("h"), tiles(w["b1"][:, :]), ALU.add).then_inc(front.free("h"), 1)
                front.wait_free(dve, b, "h")
                normalise(b, 0, gate[:, :, :], hid[:, :, :])
                done(V.tensor_tensor(hid[:, :, :], hid[:, :, :], over(stat[:, 3, :], D), ALU.mult))
                done(V.tensor_tensor(hid[:, :, :], hid[:, :, :], tiles(w["gamma"][:, :]), ALU.mult))
                V.tensor_tensor(hid[:, :, :], hid[:, :, :], tiles(w["beta"][:, :]), ALU.add).then_inc(gate_in, 1)
                yield 0
                dve.wait_ge(gate_exp, b + 1)
                done(V.tensor_scalar(gate[:, :, :], gate[:, :, :], 1.0, None, ALU.add))
                done(V.reciprocal(gate[:, :, :], gate[:, :, :]))
                V.tensor_tensor(hid[:, :, :], hid[:, :, :], gate[:, :, :], ALU.mult).then_inc(silu_ready, 1)
                yield 0
                front.wait_full(dve, b, "tok")
                V.tensor_tensor(tok[:, :, :], grid("tok"), tiles(w["b2"][:, :]), ALU.add).then_inc(front.free("tok"), 1)
                front.wait_free(dve, b, "tok")
                front.wait_full(dve, b, "silu")
                normalise(b, 1, tok[:, :, :], hid[:, :, :])
                V.tensor_tensor(hid[:, :, :], hid[:, :, :], over(stat[:, 3, :], D), ALU.mult).then_inc(ln_ready, 1)
                yield 0
                for dst, a, s, cos, sin in ((qT, "qA", "qB", "cosq", "sinq"), (kT, "kA", "kB", "cosk", "sink")):
                    front.wait_full(dve, b, a)
                    V.tensor_tensor(ropeA[:, :], front.bank(a)[0:D, :], w[cos][:, :], ALU.mult).then_inc(front.free(a), 1)
                    front.wait_full(dve, b, s)
                    V.tensor_tensor(ropeB[:, :], front.bank(s)[0:D, :], w[sin][:, :], ALU.mult).then_inc(front.free(s), 1)
                    front.wait_free(dve, b, a)
                    front.wait_free(dve, b, s)
                    if dst is qT:
                        done(V.tensor_tensor(dst[:, :], ropeA[:, :], ropeB[:, :], ALU.add))
                    else:
                        V.tensor_tensor(dst[:, :], ropeA[:, :], ropeB[:, :], ALU.add).then_inc(qk_ready, 1)
                yield from attend(front, b, 1, front_max, front_norm)
                yield 0
                front.wait_full(dve, b, "att")
                V.tensor_tensor(tok[:, :, :], grid("att"), tok[:, :, :], ALU.add).then_inc(front.free("att"), 1)
                front.wait_free(dve, b, "att")
                front.wait_full(dve, b, "ln1")
                yield 0
                normalise(b, 2, tok[:, :, :], hid[:, :, :])
                V.tensor_tensor(hid[:, :, :], hid[:, :, :], over(stat[:, 3, :], D), ALU.mult).then_inc(ln_ready, 1)

            def top(b, t):
                front.wait_free(dve, b, f"sim{t},0")
                front.wait_free(dve, b, f"sim{t},1")
                done(V.tensor_copy(fsum[:, 0, :], sim[:, t, 0:H]))

                def top16(lanes, src, vals, inds):
                    m = [mark(V.max(vals(r)[:, 0:8], src(r))) for r in range(lanes)]
                    yield 0
                    for r in range(lanes):
                        wait(m[r])
                        n = mark(V.max_index(inds(r)[:, 0:8], vals(r)[:, 0:8], src(r)))
                        m[r] = n
                    yield 0
                    for r in range(lanes):
                        wait(m[r])
                        m[r] = mark(V.match_replace(src(r), vals(r)[:, 0:8], src(r), LOW))
                    for r in range(lanes):
                        wait(m[r])
                        m[r] = mark(V.max(vals(r)[:, 8:16], src(r)))
                    for r in range(lanes):
                        wait(m[r])
                        m[r] = mark(V.max_index(inds(r)[:, 8:16], vals(r)[:, 8:16], src(r)))
                    wait(m[-1])

                yield from top16(LANES, lambda r: sim[:, t, r * NK:(r + 1) * NK], lambda r: best[:, r, :], lambda r: besti[:, r, :])
                mark(V.tensor_copy(bestf[:, 0:H, :], besti[:, 0:H, :]))
                done(V.tensor_scalar(bestf[:, H:LANES, :], besti[:, H:LANES, :], float(NK), None, ALU.mult))
                at = 0
                for a, na, nb in STAIR:
                    for src, dst in ((best, cand), (bestf, candi)):
                        n = mark(V.tensor_tensor(
                            dst[:, :, at:at + na * nb].rearrange("p h (a b) -> p h a b", b=nb),
                            src[:, 0:H, a:a + na].unsqueeze(3).to_broadcast([P, H, na, nb]),
                            src[:, H:LANES, 0:nb].unsqueeze(2).to_broadcast([P, H, na, nb]), ALU.add))
                    at += na * nb
                wait(n)
                yield from top16(H, lambda h: cand[:, h, :], lambda h: fin[:, h, :], lambda h: finp[:, h, :])
                mark(V.tensor_copy(finf[:, :, :], finp[:, :, :]))
                done(V.tensor_copy(fsum[:, 0, :], fin[:, :, 0]))
                V.tensor_tensor(fin[:, :, :], fin[:, :, :], over(fsum[:, 0, :], TOPK), ALU.subtract).then_inc(fin_ready, 1)
                for h in range(0, H, 2):
                    yield 0
                    lane = hot[:, :, :].rearrange("p (h s) n -> p h s n", h=2)
                    done(V.tensor_tensor(hot[:, :, :], over(finf[:, h:h + 2, :].rearrange("p h s -> p (h s)"), NC),
                                         w["iota"][:, :].unsqueeze(1).to_broadcast([P, 2 * TOPK, NC]), ALU.is_equal))
                    done(V.tensor_tensor(lane, lane, candi[:, h:h + 2, :].unsqueeze(2).to_broadcast([P, 2, TOPK, NC]), ALU.mult))
                    done(V.tensor_reduce(bestf[:, h:h + 2, :].rearrange("p h s -> p (h s)"), hot[:, :, :], AX.X, ALU.add))
                    V.tensor_tensor(idx[:, t, h * TOPK:(h + 2) * TOPK], bestf[:, h:h + 2, :].rearrange("p h s -> p (h s)"),
                                    w["head_base"][:, h * TOPK:(h + 2) * TOPK], ALU.add).then_inc(idx_ready, 1)
                dve.wait_ge(fin_exp, b * NT + t + 1)
                done(V.tensor_reduce(fsum[:, 0, :], fin[:, :, :], AX.X, ALU.add))
                done(V.reciprocal(fsum[:, 1, :], fsum[:, 0, :]))
                done(V.tensor_tensor(wgt[:, t, :].rearrange("p (h s) -> p h s", h=H), fin[:, :, :], over(fsum[:, 1, :], TOPK), ALU.mult))

            def combine(c, g, between):
                t, h = place(c, g)
                slot = rows[:, g % SLOTS, :, :]
                if g == 0 and not is_first(c):
                    dve.wait_ge(kv_ready, c)
                dve.wait_ge(rows_in[g % SLOTS], (c * (TILES // SLOTS) + g // SLOTS + 1) * 16 * TOPK)
                n = mark(V.tensor_tensor(slot, slot, over(wgt[:, t, h * TOPK:(h + 1) * TOPK], 2 * D), ALU.mult))
                between()
                wait(n)
                V.tensor_reduce(kv[:, t, h, :], slot.rearrange("p s n -> p n s"), AX.X, ALU.add).then_inc(slot_free, 1)

            def keep(c):
                done(V.tensor_copy(tok_cur[:, :, :], tok[:, :, :]))

            def run_back(c):
                if is_last(c):
                    yield from attend(back, c, H, back_max, back_norm, lambda h: (h + 1) * NT)
                else:
                    yield from attend(back, c, H, back_max, back_norm)
                yield 0
                back.wait_full(dve, c, "out")
                dve.wait_ge(y_out, c * 16 + 16)
                V.tensor_tensor(y[:, :, :], back.bank("out")[:, 0:NT * D].rearrange("p (t n) -> p t n", n=D), tok_cur[:, :, :], ALU.add).then_inc(back.free("out"), 1)
                back.wait_free(dve, c, "out")

            def prepare_next(c):
                keep(c)
                yield from run_front(c + 1)

            def weave(c, others, pace):
                need = [next(others)]

                def step(g):
                    if need[0] is not None and g >= need[0]:
                        need[0] = next(others, None)

                for g in range(TILES):
                    def between():
                        for _ in range(pace(g)):
                            step(g)
                    combine(c, g, between)
                while need[0] is not None:
                    step(TILES)
                section_end()

            def run(*parts):
                for part in parts:
                    yield 0
                    yield from part

            def next_tops(c):
                for t in range(NT):
                    yield (t + 1) * H
                    yield from top(c + 1, t)

            def body(c):
                if is_first(c):
                    weave(c, run(top(0, 1), top(0, 2), top(0, 3), prepare_next(c), next_tops(c)), lambda g: PACE[g // H])
                elif is_last(c):
                    weave(c, run(run_back(c - 1), last_back(c)), lambda g: PACE_LAST)
                else:
                    weave(c, run(run_back(c - 1), prepare_next(c), next_tops(c)), lambda g: PACE[g // H])

            def last_back(c):
                keep(c)
                yield NT
                yield from run_back(c)

            V.memset(y[:, :, :], 0.0).then_inc(slot_free, SLOTS)
            dve.wait_ge(weights_in, NW)
            for _ in run(run_front(0), top(0, 0)):
                pass
            section_end()
            body(0)
            with dve.Fori(1, NB - 1) as c:
                body(c)
            body(NB - 1)


def kernel(**inputs):
    import numpy as np
    import concourse.bacc as bacc
    from concourse.bass_utils import run_bass_kernel_spmd as run

    f = np.float32
    a = {k: np.asarray(v) for k, v in inputs.items()}

    def rep(v):
        return np.ascontiguousarray(np.broadcast_to(v.reshape(1, -1), (P, v.size)))

    n_rope = D // 4
    rot = np.arange(n_rope) ^ 1
    half = n_rope // 2
    theta = (f(1.0) / (f(10000.0) ** (np.arange(half, dtype=f) / f(half)))).astype(f)
    angle = np.arange(T, dtype=f)[:, None] * theta[None, :]
    cos, sin = np.ones((D, T), f), np.zeros((D, T), f)
    cos[D - n_rope:] = np.repeat(np.cos(angle).T, 2, axis=0)
    sin[D - n_rope:] = np.repeat(np.sin(angle).T, 2, axis=0)
    sin[D - n_rope::2] *= f(-1.0)
    scale = f(D ** -0.5)
    pk = a["L0_ffn_pk_keys"]
    keys = np.zeros((4, P, 4, NK), f)
    for s in range(2):
        for h in range(H):
            keys[2 * s + h // 4, (h % 4) * 32:(h % 4 + 1) * 32, h % 4, :] = pk[s, :, h, :].T
    d = {
        "x": a["x"].view(np.uint32).reshape(NB, NT, P).transpose(0, 2, 1), "adj": a["mask_BSS_b0_1"], "rel": a["fside_BSS_rel_dist"],
        "embed": np.concatenate([a["L0_tok_atom_embed"], a["L0_tok_neighbor_embed"]], axis=1),
        "table": np.concatenate([a["L0_ffn_keys_table"], a["L0_ffn_values_table"]], axis=1),
        "ident": np.eye(P, dtype=f), "noteye": (1 - np.eye(P)).astype(f),
        "causal": np.triu(np.full((P, P), LOW, f), 1),
        "iota": rep(np.arange(NC, dtype=f)), "head_base": rep(np.repeat(np.arange(H, dtype=f) * NK * NK, TOPK)),
        "cosq": cos * scale, "sinq": sin * scale, "cosk": cos, "sink": sin,
        "wrd": a["L0_tok_w_rd"].reshape(D, 1), "w1": a["L0_tok_w1"], "b1": rep(a["L0_tok_b1"]),
        "gamma": rep(a["L0_tok_gamma"]), "beta": rep(a["L0_tok_beta"]), "w2": a["L0_tok_w2"], "b2": rep(a["L0_tok_b2"]),
        "wcomp": np.concatenate([a["L0_attn_Wq_comp"], a["L0_attn_Wkv_comp"]], axis=1),
        "wq_a": np.concatenate([a["L0_attn_Wqc"], a["L0_attn_Wqr"]], axis=1),
        "wq_b": np.concatenate([a["L0_attn_Wqc"], a["L0_attn_Wqr"][:, rot]], axis=1),
        "wk_a": np.concatenate([a["L0_attn_Wkc"], a["L0_attn_Wkr"]], axis=1),
        "wk_b": np.concatenate([a["L0_attn_Wkc"], a["L0_attn_Wkr"][:, rot]], axis=1),
        "wv": a["L0_attn_Wv"], "wpk": a["L0_ffn_Wq_pk"], "wq": a["L0_ffn_Wq"],
        "keys": keys.transpose(1, 0, 2, 3).reshape(P, 4 * 4 * NK),
        "wo": a["L0_ffn_Wo"].reshape(H, D, D).transpose(1, 0, 2).reshape(D, H * D),
    }
    d = {k: np.ascontiguousarray(v) for k, v in d.items()}
    nc = bacc.Bacc("TRN2", target_bir_lowering=False, num_devices=1)
    aps = {k: nc.dram_tensor("in_" + k, v.shape, mybir.dt.from_np(v.dtype), kind="ExternalInput").ap() for k, v in d.items()}
    out = nc.dram_tensor("out", (NB, T, D), F32, kind="ExternalOutput").ap()
    tower(nc, aps, out)
    r = run(nc, [{"in_" + k: v for k, v in d.items()}], core_ids=[0])
    return r.results[0]["out"]
```

```python
import concourse.bass as bass
from concourse import mybir
from contextlib import ExitStack

F32 = mybir.dt.float32
BF16 = mybir.dt.bfloat16
U32 = mybir.dt.uint32
U8 = mybir.dt.uint8
U16 = mybir.dt.uint16
ALU = mybir.AluOpType
ACT = mybir.ActivationFunctionType
AX = mybir.AxisListType

P = 128
NB, T, D = 8, 512, 64
NT = T // P
H = 8
DH = 2
GH = H - DH
NK = 64
TOPK = 16
LANES = 2 * H
SLOTS = 4
EPS = 1e-5
LOW = -3.0e38

STAIR = [(0, 1, 16), (1, 1, 8), (2, 2, 5), (4, 4, 3), (8, 8, 1)]
NCHUNK = NK * NK // P
GROUP = 4
RING = 2
HOTS_AT = 5
TOP_STEPS = HOTS_AT + DH + GH // 2 + 1
FRONT_DENSE = (1, 2)
BACK_TOPS = (2, 1)
PACE_FIRST = [7] * 9 + [9] * 9 + [6] * 6
PACE = [9] * 10 + [8] * 14
PACE_LAST = [8] * (NT * GH)
NC = sum(na * nb for _, na, nb in STAIR)


class Phase:

    def __init__(self, plan, full, free, banks):
        self.uses, self.at = {}, {}
        self.full_sem, self.free_sem, self.banks = full, free, banks
        for step, bank in plan:
            self.at[step] = (bank, self.uses.get(bank, 0))
            self.uses[bank] = self.uses.get(bank, 0) + 1

    def bank(self, step):
        return self.banks[self.at[step][0]]

    def full(self, step):
        return self.full_sem[self.at[step][0]]

    def free(self, step):
        return self.free_sem[self.at[step][0]]

    def wait_full(self, eng, b, step):
        bank, n = self.at[step]
        eng.wait_ge(self.full_sem[bank], b * self.uses[bank] + n + 1)

    def wait_free(self, eng, b, step):
        bank, n = self.at[step]
        eng.wait_ge(self.free_sem[bank], b * self.uses[bank] + n + 1)

    def wait_room(self, eng, b, step):
        bank, n = self.at[step]
        if n:
            eng.wait_ge(self.free_sem[bank], b * self.uses[bank] + n)

    def wait_all_free(self, eng, b):
        for bank, k in self.uses.items():
            eng.wait_ge(self.free_sem[bank], b * k + k)


def attention_plan():
    plan = [("q0", "M"), ("k0", "M"), ("q1", "M")]
    for h in range(H + 1):
        if h < H:
            plan += [(f"S{h},{i}", f"S{i % 2}") for i in range(NT)]
            plan += [(f"P{h},{i}", "T") for i in range(NT)]
        if h + 1 < H:
            plan += [(f"k{h + 1}", "M")]
        if h:
            plan += [(f"o{h - 1}", "M")]
        if h + 2 < H:
            plan += [(f"q{h + 2}", "M")]
    return plan


def attention_steps(heads, first, second, prelude):
    prelude()
    yield 0
    for n in range(heads * NT + 2):
        first(n)
        yield 0
        second(n)
        yield 0


FRONT = ([("rel0", "T"), ("rel1", "M"), ("rel2", "S0"), ("rel3", "S1"),
          ("emb", "T"), ("nbr", "O"), ("h", "M"), ("silu", "T"), ("tok", "O"), ("ln1", "T"),
          ("comp", "M"), ("qA", "S0"), ("qB", "S1"), ("kA", "O"), ("kB", "M"), ("v", "T")]
         + [(f"S0,{i}", f"S{i % 2}") for i in range(NT)] + [(f"P0,{i}", "T") for i in range(NT)]
         + [("o0", "O"), ("att", "M"), ("ln2", "T")]
         + [(f"qpk{m}", bank) for m, bank in enumerate(["M", "S0", "S1", "O"])]
         + [(f"sim{t},{s}", ["T", "M", "S0", "S1", "O"][(2 * t + s) % 5]) for t in range(NT) for s in range(2)])
BACK = attention_plan() + [("out", "O")]
DENSE = [use for d in range(DH) for use in
         [(f"{x}{d},{m}", x) for m in range(NCHUNK) for x in ("L", "D")] + [(f"acc{d}", "A"), (f"kv{d}", "A")]]
RANKS = [("stair0", "L"), ("stair1", "D")] + [(f"log{t}", "A") for t in range(NT)]


def merge(a, b, na=1, nb=1):
    ends = object()
    parts = [[a, next(a), na], [b, next(b), nb]]
    while parts:
        for part in list(parts):
            for _ in range(part[2]):
                yield part[1]
                part[1] = next(part[0], ends)
                if part[1] is ends:
                    parts.remove(part)
                    break


def drain(steps):
    for _ in steps:
        pass


def tower(nc, d, out):
    ctx = ExitStack()
    with ctx:
        def sb(name, shape, dt=F32):
            return ctx.enter_context(nc.sbuf_tensor(name, shape, dt))

        def sem(name):
            return ctx.enter_context(nc.semaphore(name))

        CONST = ["ident", "noteye", "causal", "iota", "head_base", "w1", "b1", "gamma", "beta", "b2"]
        K64 = ["cosq", "sinq", "cosk", "sink", "w2", "wcomp", "wq", "wpk", "wo"]
        HIGH = ["wrd", "wk_a", "wk_b", "wv"]
        w = {n: sb(n, list(d[n].shape)) for n in CONST + K64 + ["wq_a", "wq_b", "keys"]}
        for n in HIGH:
            w[n] = sb(n, [P, d[n].shape[1]])
        ids = sb("ids", [P, NT], U32)
        rel = sb("rel", [P, NT, T])
        adj = sb("adj", [P, NT, T], U8)
        emb = sb("emb", [P, NT, 2 * D])
        wide = sb("wide", [P, NT, T])
        relT = wide[:, :, :]
        qpkT = wide[:, :, :]
        probT = wide[:, :, :]
        xT = sb("xT", [P, T])
        compT = xT[:, :]
        hid = sb("hid", [P, NT, D])
        sq = sb("sq", [P, NT, D])
        gate = sb("gate", [P, NT, D])
        stat = sb("stat", [P, 4, NT])
        tok = sb("tok", [P, NT, D])
        lnT = sb("lnT", [D, T])
        actT = lnT[:, :]
        qT = sb("qT", [D, T])
        kT = sb("kT", [D, T])
        val = sb("val", [P, NT, D])
        sim = sb("sim", [P, NT, LANES * NK])
        prob = [sb(f"prob{i}", [P, T]) for i in range(2)]
        ropeA, ropeB = prob[0][0:D, :], prob[1][0:D, :]
        negmax = sb("negmax", [P, 2])
        psum = sb("psum", [P, 2])
        pinv = sb("pinv", [P, 2])
        oT = sb("oT", [D, T])
        best = sb("best", [P, LANES, TOPK])
        besti = sb("besti", [P, LANES, TOPK], U32)
        bestf = sb("bestf", [P, LANES, TOPK])
        cand = sb("cand", [P, H, NC])
        candi = sb("candi", [P, H, NC], U16)
        fin = sb("fin", [P, H, TOPK])
        finp = sb("finp", [P, H, TOPK], U32)
        finf = sb("finf", [P, H, TOPK])
        hot = sb("hot", [P, 2 * TOPK, NC], U16)
        key_at = sb("key_at", [P, NK, TOPK], BF16)
        best16 = sb("best16", [P, 2, DH, TOPK], BF16)
        worth = sb("worth", [P, DH, 2, TOPK], BF16)
        fsum = sb("fsum", [P, 2, H])
        ident16 = sb("ident16", [P, P], BF16)
        spread = sb("spread", [P, NCHUNK, P], BF16)
        logs = sb("logs", [P, DH, 2, NK])
        picked = sb("picked", [P, DH, NC])
        hots = [rel[:, 2 * d:2 * d + 2, :].rearrange("p a n -> p (a n)").bitcast(BF16).rearrange("p (n a) -> p n a", a=TOPK)
                for d in range(DH)]
        stairT = sb("stairT", [P, DH, T], BF16)
        parts = [sb(f"part{i}", [P, DH, T], BF16) for i in range(3)]
        dprob = [sb(f"dprob{i}", [P, T]) for i in range(3)]
        rest = dprob[0][:, 0:DH * P].rearrange("p (h n) -> p h n", h=DH)
        kvT = sb("kvT", [P, T])
        block_rows = sb("block_rows", [P, RING, GROUP, 2 * D])
        inv = sb("inv", [P, NT, DH])
        idx = sb("idx", [P, NT, GH * TOPK], U32)
        wgt = sb("wgt", [P, NT, GH * TOPK])
        rows = sb("rows", [P, SLOTS, TOPK, 2 * D])
        kv = sb("kv", [P, NT, H, 2 * D])
        kv_cur = sb("kv_cur", [P, NT, H, 2 * D])
        lnT_mid, lnT_cur = sb("lnT_mid", [D, T]), sb("lnT_cur", [D, T])
        tok_mid, tok_cur = sb("tok_mid", [P, NT, D]), sb("tok_cur", [P, NT, D])
        khT = [sb(f"khT{i}", [D, T]) for i in range(2)]
        qhT = [sb(f"qhT{i}", [D, T]) for i in range(2)]
        y = sb("y", [P, NT, D])

        names = ["T", "M", "S0", "S1", "O", "L", "D", "A"]
        banks = {n: ctx.enter_context(nc.psum_tensor(n, [P, 512], F32)) for n in names}
        front = Phase(FRONT, {n: sem("front_full_" + n) for n in names[:5]},
                      {n: sem("front_free_" + n) for n in names[:5]}, banks)
        back = Phase(BACK, {n: sem("back_full_" + n) for n in names[:5]},
                     {n: sem("back_free_" + n) for n in names[:5]}, banks)

        dense = Phase(DENSE, {n: sem("dense_full_" + n) for n in names[5:]},
                      {n: sem("dense_free_" + n) for n in names[5:]}, banks)
        ranks = Phase(RANKS, {n: sem("ranks_full_" + n) for n in names[5:]},
                      {n: sem("ranks_free_" + n) for n in names[5:]}, banks)
        spread_ready = sem("spread_ready")
        hot_ready, hot_used = sem("hot_ready"), sem("hot_used")
        high_done, mid_done, parts_ready = sem("high_done"), sem("mid_done"), sem("parts_ready")
        blocks_in = [sem(f"blocks_in{i}") for i in range(RING)]
        block_used = sem("block_used")
        weights_in, rel_in, adj_in, ids_in = sem("weights_in"), sem("rel_in"), sem("adj_in"), sem("ids_in")
        emb_in = sem("emb_in")
        rel_masked = sem("rel_masked")
        var_ready, rstd_ready, log_done = sem("var_ready"), sem("rstd_ready"), sem("log_done")
        gate_in, gate_exp = sem("gate_in"), sem("gate_exp")
        silu_ready = sem("silu_ready")
        ln_ready = sem("ln_ready")
        qk_ready = sem("qk_ready")
        front_max, front_inverse, front_norm = sem("front_max"), sem("front_inverse"), sem("front_norm")
        back_max, back_inverse, back_norm = sem("back_max"), sem("back_inverse"), sem("back_norm")
        fin_ready, fin_exp = sem("fin_ready"), sem("fin_exp")
        idx_ready = sem("idx_ready")
        scaled = sem("scaled")
        slot_free = sem("slot_free")
        rows_in = [sem(f"rows_in{i}") for i in range(SLOTS)]
        mid_ready, cur_ready = sem("mid_ready"), sem("cur_ready")
        tok_ready = sem("tok_ready")
        kv_ready = sem("kv_ready")
        y_out = sem("y_out")
        pe_holds, pool_holds, dve_holds, sp_holds = sem("pe_holds"), sem("pool_holds"), sem("dve_holds"), sem("sp_holds")
        vec = sem("vec")

        NW = 16 * len(w)
        TILES = NT * GH
        block = ctx.enter_context(nc.Block())

        order = ["ident", "noteye"] + [n for n in w if n not in ("ident", "noteye")]

        def load_weights(eng, names):
            for n in names:
                dst = w[n][:, :] if n not in HIGH else w[n][D:P, :]
                eng.dma_start(dst, d[n]).then_inc(weights_in, 16)

        def place(c, g):
            t, h = (g % NT, g // NT) if is_last(c) else divmod(g, GH)
            return t, DH + h

        def is_last(c):
            return isinstance(c, int) and c == NB - 1

        def is_over(c):
            return isinstance(c, int) and c == NB

        def is_first(b):
            return isinstance(b, int) and b == 0

        def logs_of(t):
            return ranks.bank(f"log{t}")[:, 0:DH * P].rearrange("p (h n) -> p h n", h=DH)

        def run(*phases):
            for phase in phases:
                yield 0
                yield from phase

        def body_steps(c, front, dense, top, back, kept):
            def next_tops():
                for t in range(NT):
                    yield from top(c + 1, t, (t + 1) * GH)

            def last_back():
                for k, _ in enumerate(back(c)):
                    h = (k + 3) // (2 * NT) + 1
                    yield min(TILES, max(0, (h - DH + 1) * NT))

            if is_first(c):
                return run(top(0, 1), top(0, 2), top(0, 3), kept(c), merge(front(c + 1), dense(c), *FRONT_DENSE), next_tops())
            if is_last(c):
                return run(kept(c), merge(back(c - 1), dense(c)), kept(c + 1), last_back())
            return run(kept(c), merge(front(c + 1), dense(c), *FRONT_DENSE), merge(back(c - 1), next_tops(), *BACK_TOPS))

        def weave(c, others, before, after):
            pace = PACE_FIRST if is_first(c) else PACE_LAST if is_last(c) else PACE
            need = next(others)
            for g in range(TILES):
                before(c, g)
                for _ in range(pace[g]):
                    if need is not None and g >= need:
                        need = next(others, None)
                after(c, g)
            while need is not None:
                need = next(others, None)

        def hold(eng, own):
            eng.sem_inc(own, 1)

        @block.sync
        def _(sp):
            def load(b):
                one = bass.ds(b, 1)
                if not is_first(b):
                    front.wait_full(sp, b - 1, "rel3")
                    sp.wait_ge(emb_in, (b - 1) * 64 + 64)
                sp.dma_start(ids[:, :], d["x"][one, :, :].rearrange("b p t -> p (b t)")).then_inc(ids_in, 16)
                sp.dma_start(adj[:, :, :], d["adj"][one, :, :].rearrange("b (t p) j -> p (b t) j", p=P)).then_inc(adj_in, 16)
                if not is_first(b):
                    sp.wait_ge(hot_used, b * NT * DH)
                    hold(sp, sp_holds)
                sp.dma_start(rel[:, :, :], d["rel"][one, :, :].rearrange("b (t p) j -> p (b t) j", p=P)).then_inc(rel_in, 16)

            def store(b):
                back.wait_free(sp, b, "out")
                one = bass.ds(b, 1)
                sp.dma_start(out[one, :, :].rearrange("b (t p) n -> p (b t) n", p=P), y[:, :, :]).then_inc(y_out, 16)

            LOADS = NCHUNK // GROUP

            def stream(c):
                for n in range(DH * LOADS):
                    if n >= RING or not is_first(c):
                        sp.wait_ge(block_used, c * DH * NCHUNK + (n - RING + 1) * GROUP)
                    at = (n // LOADS) * NK * NK + (n % LOADS) * GROUP * P
                    sp.dma_start(block_rows[:, n % RING, :, :],
                                 d["table"][at:at + GROUP * P, :].rearrange("(k p) n -> p k n", p=P)).then_inc(blocks_in[n % RING], 16)

            sp.sem_inc(y_out, 16)
            load(0)
            load_weights(sp, order[0::2])
            load(1)
            stream(0)
            with sp.Fori(1, NB - 1) as c:
                load(c + 1)
                stream(c)
                store(c - 1)
            stream(NB - 1)
            store(NB - 2)
            store(NB - 1)
            sp.wait_ge(y_out, 16 * NB + 16)

        @block.gpsimd
        def _(pool):
            def gather_embeddings(b):
                pool.wait_ge(ids_in, b * 16 + 16)
                if not is_first(b):
                    front.wait_full(pool, b - 1, "nbr")
                    front.wait_full(pool, b - 1, "emb")
                hold(pool, pool_holds)
                for t in range(NT):
                    pool.indirect_dma_start(emb[:, t, :], None, d["embed"], bass.IndirectOffsetOnAxis(ids[:, t:t + 1], 0)).then_inc(emb_in, 16)

            def gather_rows(c):
                for g in range(TILES):
                    if g == 1 and not is_last(c):
                        gather_embeddings(c + 1)
                    t, h = place(c, g)
                    if h % 2 == 0:
                        pool.wait_ge(idx_ready, (c * NT + t) * (GH // 2) + (h - DH) // 2 + 1)
                    pool.wait_ge(slot_free, c * TILES + g + 1)
                    hold(pool, pool_holds)
                    at = (h - DH) * TOPK
                    for s in range(TOPK):
                        pool.indirect_dma_start(rows[:, g % SLOTS, s, :], None, d["table"],
                                                bass.IndirectOffsetOnAxis(idx[:, t, at + s:at + s + 1], 0)).then_inc(rows_in[g % SLOTS], 16)

            gather_embeddings(0)
            with pool.Fori(0, NB - 1) as c:
                gather_rows(c)
            gather_rows(NB - 1)

        @block.tensor
        def _(pe):
            mm = nc.tensor.matmul

            def transposes(ph, b, step, parts, width):
                ph.wait_room(pe, b, step)
                if width < P:
                    hold(pe, pe_holds)
                for t, a in enumerate(parts):
                    last = nc.tensor.transpose(ph.bank(step)[0:width, t * P:(t + 1) * P], a, w["ident"][:, :])
                last.then_inc(ph.full(step), 1)

            def attend(ph, b, heads, fetch, queries, keys, values, norm, project=None):
                N = heads * NT

                def scores(n):
                    h, i = divmod(n, NT)
                    if i == 0 and fetch is not None:
                        ph.wait_free(pe, b, f"k{h}")
                        ph.wait_free(pe, b, f"q{h}")
                    step = f"S{h},{i}"
                    ph.wait_room(pe, b, step)
                    m = (i + 1) * P
                    mm(ph.bank(step)[:, 0:m], queries(h)[:, i * P:(i + 1) * P], keys(h)[:, 0:m], start=True, stop=False)
                    mm(ph.bank(step)[:, i * P:m], w["ident"][:, :], w["causal"][:, :], start=False, stop=True).then_inc(ph.full(step), 1)

                def output(h):
                    ph.wait_free(pe, b, f"P{h},{NT - 1}")
                    ph.wait_room(pe, b, f"o{h}")
                    for k in range(NT):
                        last = mm(ph.bank(f"o{h}")[0:D, k * P:], values(h, k), probT[:, k, k * P:],
                                  start=(k == 0), stop=(k == NT - 1))
                    last.then_inc(ph.full(f"o{h}"), 1)

                def prelude():
                    if fetch is not None:
                        for what, h in (("q", 0), ("k", 0), ("q", 1)):
                            fetch(h, what)
                    scores(0)
                    scores(1)

                def first(n):
                    if 1 <= n <= N:
                        h, i = divmod(n - 1, NT)
                        pe.wait_ge(norm, b * N + n)
                        transposes(ph, b, f"P{h},{i}", [prob[i % 2][:, k * P:(k + 1) * P] for k in range(i + 1)], P)
                    if n + 2 < N:
                        scores(n + 2)

                def second(n):
                    h, i = divmod(n, NT)
                    if i == 0 and h + 1 < heads:
                        fetch(h + 1, "k")
                    elif i == 1 and h:
                        output(h - 1)
                    elif i == 2 and h and project is not None:
                        project(h - 1)
                    elif i == 3 and h + 2 < heads:
                        fetch(h + 2, "q")

                yield from attention_steps(heads, first, second, prelude)

            def run_front(b):
                yield 0
                pe.wait_ge(rel_masked, b + 1)
                for j in range(NT):
                    transposes(front, b, f"rel{j}", [rel[:, t, j * P:(j + 1) * P] for t in range(NT)], P)
                pe.wait_ge(emb_in, b * 64 + 64)
                transposes(front, b, "emb", [emb[:, t, :] for t in range(NT)], P)
                yield 0
                for j in range(NT):
                    front.wait_free(pe, b, f"rel{j}")
                for j in range(NT):
                    last = mm(front.bank("nbr")[:, :], emb[:, j, :], relT[:, j, :], start=(j == 0), stop=(j == NT - 1))
                last.then_inc(front.full("nbr"), 1)
                yield 0
                front.wait_free(pe, b, "emb")
                front.wait_free(pe, b, "nbr")
                front.wait_room(pe, b, "h")
                for t in range(NT):
                    last = mm(front.bank("h")[:, t * D:(t + 1) * D], xT[:, t * P:(t + 1) * P], w["w1"][:, :], start=True, stop=True)
                last.then_inc(front.full("h"), 1)
                for _ in range(4):
                    yield 0
                pe.wait_ge(silu_ready, b + 1)
                transposes(front, b, "silu", [hid[:, t, :] for t in range(NT)], D)
                yield 0
                front.wait_free(pe, b, "silu")
                front.wait_room(pe, b, "tok")
                for t in range(NT):
                    last = mm(front.bank("tok")[:, t * D:(t + 1) * D], actT[:, t * P:(t + 1) * P], w["w2"][:, :], start=True, stop=True)
                last.then_inc(front.full("tok"), 1)
                yield 0
                yield 0
                pe.wait_ge(ln_ready, b * 2 + 1)
                transposes(front, b, "ln1", [hid[:, t, :] for t in range(NT)], D)
                yield 0
                front.wait_free(pe, b, "ln1")
                front.wait_room(pe, b, "comp")
                mm(front.bank("comp")[:, :], w["wcomp"][:, :], lnT[:, :], start=True, stop=True).then_inc(front.full("comp"), 1)
                yield 0
                front.wait_free(pe, b, "comp")
                for step, lhs, lo in (("qA", "wq_a", 0), ("qB", "wq_b", 0), ("kA", "wk_a", D), ("kB", "wk_b", D)):
                    front.wait_room(pe, b, step)
                    hold(pe, pe_holds)
                    mm(front.bank(step)[0:D, :], w[lhs][lo:lo + D, :], compT[lo:lo + D, :], start=True, stop=True).then_inc(front.full(step), 1)
                front.wait_room(pe, b, "v")
                hold(pe, pe_holds)
                for t in range(NT):
                    last = mm(front.bank("v")[:, t * D:(t + 1) * D], compT[D:P, t * P:(t + 1) * P], w["wv"][D:P, :], start=True, stop=True)
                last.then_inc(front.full("v"), 1)
                yield 0
                yield 0
                pe.wait_ge(qk_ready, b + 1)
                front.wait_free(pe, b, "v")
                yield from attend(front, b, 1, None, lambda h: qT, lambda h: kT, lambda h, k: val[:, k, :], front_norm)
                front.wait_free(pe, b, "o0")
                front.wait_room(pe, b, "att")
                for t in range(NT):
                    last = mm(front.bank("att")[:, t * D:(t + 1) * D], oT[:, t * P:(t + 1) * P], w["ident"][0:D, 0:D], start=True, stop=True)
                last.then_inc(front.full("att"), 1)
                yield 0
                yield 0
                pe.wait_ge(ln_ready, b * 2 + 2)
                transposes(front, b, "ln2", [hid[:, t, :] for t in range(NT)], D)
                yield 0
                front.wait_free(pe, b, "ln2")
                for m in range(4):
                    front.wait_room(pe, b, f"qpk{m}")
                    mm(front.bank(f"qpk{m}")[:, :], w["wpk"][:, m * P:(m + 1) * P], lnT[:, :], start=True, stop=True).then_inc(front.full(f"qpk{m}"), 1)
                yield 0
                for m in range(4):
                    front.wait_free(pe, b, f"qpk{m}")
                for t in range(NT):
                    for s in range(2):
                        front.wait_room(pe, b, f"sim{t},{s}")
                        for g in range(2):
                            m = 2 * s + g
                            last = mm(front.bank(f"sim{t},{s}")[:, g * 256:(g + 1) * 256], qpkT[:, m, t * P:(t + 1) * P],
                                      w["keys"][:, m * 256:(m + 1) * 256], start=True, stop=True)
                        last.then_inc(front.full(f"sim{t},{s}"), 1)
                    yield 0
                front.wait_all_free(pe, b)

            def run_back(c):
                src = kv if is_last(c) else kv_cur
                pe.wait_ge(cur_ready, c + 1)
                pe.wait_ge(tok_ready, c + 1)
                mm(back.bank("out")[:, 0:NT * D], w["ident"][:, :], tok_cur[:, :, :].rearrange("p t n -> p (t n)"), start=True, stop=False)
                if not is_last(c):
                    pe.wait_ge(kv_ready, c + 1)

                def fetch(h, what):
                    back.wait_room(pe, c, f"{what}{h}")
                    if what == "q":
                        hold(pe, pe_holds)
                        mm(back.bank(f"q{h}")[0:D, :], w["wq"][:, h * D:(h + 1) * D], lnT_cur[:, :], start=True, stop=True).then_inc(back.full(f"q{h}"), 1)
                        return
                    if is_last(c) and h >= DH:
                        pe.wait_ge(slot_free, c * TILES + (h - DH + 1) * NT + SLOTS)
                    elif is_last(c):
                        dense.wait_free(pe, c, f"kv{h}")
                    transposes(back, c, f"k{h}", [src[:, t, h, :] for t in range(NT)], P)

                def project(h):
                    back.wait_free(pe, c, f"o{h}")
                    for t in range(NT):
                        last = mm(back.bank("out")[:, t * D:(t + 1) * D], oT[:, t * P:(t + 1) * P], w["wo"][:, h * D:(h + 1) * D],
                                  start=False, stop=(h == H - 1 and t == NT - 1))
                    if h == H - 1:
                        last.then_inc(back.full("out"), 1)

                yield from attend(back, c, H, fetch, lambda h: qhT[h % 2], lambda h: khT[h % 2], lambda h, k: src[:, k, h, D:2 * D], back_norm, project)
                project(H - 1)
                back.wait_all_free(pe, c)

            def run_ranks(b, t, need=0):
                for k in range(TOP_STEPS):
                    if HOTS_AT <= k - 1 < HOTS_AT + DH:
                        hd = k - 1 - HOTS_AT
                        if hd == 0:
                            ranks.wait_room(pe, b, f"log{t}")
                        pe.wait_ge(hot_ready, b * NT * DH + t * DH + hd + 1)
                        last = nc.tensor.transpose(ranks.bank(f"log{t}")[:, hd * P:(hd + 1) * P],
                                                   logs[:, hd, :, :].rearrange("p s k -> p (s k)"), w["ident"][:, :])
                        if hd == DH - 1:
                            last.then_inc(ranks.full(f"log{t}"), 1)
                        for a in range(TOPK):
                            last = mm(ranks.bank(f"stair{hd}")[:, t * P:(t + 1) * P], hots[hd][:, :, a], ident16[:, :],
                                      start=(a == 0), stop=(a == TOPK - 1))
                        last.then_inc(hot_used, 1)
                    if t == NT - 1 and k == HOTS_AT + DH + 1:
                        pe.wait_ge(hot_used, b * NT * DH + NT * DH)
                        for hd in range(DH):
                            pe.sem_inc(ranks.full(f"stair{hd}"), 1)
                    if t == NT - 1 and k == TOP_STEPS - 1:
                        ranks.wait_all_free(pe, b)
                    yield 0

            def run_dense(c):
                pe.wait_ge(parts_ready, c * NT + NT)
                LOADS = NCHUNK // GROUP
                for n in range(DH * NCHUNK + 3):
                    hd, m = divmod(n, NCHUNK)
                    v = n - 2
                    headed = v > 0 and v % NCHUNK == 0
                    if headed:
                        pe.wait_ge(block_used, c * DH * NCHUNK + v)
                        pe.sem_inc(dense.full(f"acc{v // NCHUNK - 1}"), 1)
                    if n < DH * NCHUNK:
                        dense.wait_room(pe, c, f"L{hd},{m}")
                        for i in range(3):
                            last = mm(dense.bank(f"L{hd},{m}")[:, :], spread[:, m, :], parts[i][:, hd, :], start=(i == 0), stop=(i == 2))
                        last.then_inc(dense.full(f"L{hd},{m}"), 1)
                    if headed:
                        done = v // NCHUNK - 1
                        dense.wait_free(pe, c, f"acc{done}")
                        transposes(dense, c, f"kv{done}", [kvT[:, t * P:(t + 1) * P] for t in range(NT)], P)
                    if 0 <= v < DH * NCHUNK:
                        vh, vm = divmod(v, NCHUNK)
                        load, k = divmod(v, GROUP)
                        if k == 0:
                            pe.wait_ge(blocks_in[load % RING], (c * (DH * LOADS // RING) + load // RING + 1) * 16)
                        if vm == 0:
                            dense.wait_room(pe, c, f"acc{vh}")
                        dense.wait_free(pe, c, f"D{vh},{vm}")
                        mm(dense.bank(f"acc{vh}")[:, :], block_rows[:, load % RING, k, :], dprob[v % 3][:, :],
                           start=(vm == 0), stop=(vm == NCHUNK - 1)).then_inc(block_used, 1)
                    if n < DH * NCHUNK:
                        dense.wait_room(pe, c, f"D{hd},{m}")
                        mm(dense.bank(f"D{hd},{m}")[:, :], spread[:, m, :], stairT[:, hd, :], start=True, stop=True).then_inc(dense.full(f"D{hd},{m}"), 1)
                    yield 0
                dense.wait_all_free(pe, c)

            pe.wait_ge(weights_in, NW)
            def body(c):
                drain(body_steps(c, run_front, run_dense, run_ranks, run_back, lambda c: iter([0])))

            drain(run_front(0))
            drain(run_ranks(0, 0))
            body(0)
            with pe.Fori(1, NB - 1) as c:
                body(c)
            body(NB - 1)

        @block.scalar
        def _(act):
            fn = nc.scalar.activation

            def copy(ph, b, step, dst, src, scale=1.0):
                ph.wait_full(act, b, step)
                fn(dst, src, ACT.Copy, scale=scale).then_inc(ph.free(step), 1)

            def rstd(b, n):
                act.wait_ge(var_ready, b * 3 + n + 1)
                fn(stat[:, 2, :], stat[:, 1, :], ACT.Ln).then_inc(log_done, 1)
                act.wait_ge(log_done, b * 3 + n + 1)
                fn(stat[:, 3, :], stat[:, 2, :], ACT.Exp, scale=-0.5).then_inc(rstd_ready, 1)

            def attend(ph, b, heads, fetch, norm_max, inverse, norm):
                N = heads * NT

                def exps(n):
                    h, i = divmod(n, NT)
                    if n >= 2:
                        ph.wait_full(act, b, "P%d,%d" % divmod(n - 2, NT))
                    act.wait_ge(norm_max, b * N + n + 1)
                    m = (i + 1) * P
                    fn(prob[i % 2][:, 0:m], ph.bank(f"S{h},{i}")[:, 0:m], ACT.Exp, bias=negmax[:, i % 2:i % 2 + 1],
                       accum_out=psum[:, i % 2:i % 2 + 1]).then_inc(ph.free(f"S{h},{i}"), 1)

                def prelude():
                    if fetch is not None:
                        for what, h in (("q", 0), ("k", 0), ("q", 1)):
                            fetch(h, what)
                    exps(0)

                def first(n):
                    if n + 1 < N:
                        exps(n + 1)

                def second(n):
                    h, i = divmod(n, NT)
                    if n < N:
                        act.wait_ge(inverse, b * N + n + 1)
                        m = (i + 1) * P
                        fn(prob[i % 2][:, 0:m], prob[i % 2][:, 0:m], ACT.Copy, scale=pinv[:, i % 2:i % 2 + 1]).then_inc(norm, 1)
                    if i == 0 and h + 1 < heads:
                        fetch(h + 1, "k")
                    elif i == 1 and h:
                        copy(ph, b, f"o{h - 1}", oT[:, :], ph.bank(f"o{h - 1}")[0:D, :])
                    elif i == 3 and h + 2 < heads:
                        fetch(h + 2, "q")
                    if 1 <= n <= N:
                        h, i = divmod(n - 1, NT)
                        step = f"P{h},{i}"
                        copy(ph, b, step, probT[:, 0:i + 1, i * P:(i + 1) * P],
                             ph.bank(step)[:, 0:(i + 1) * P].rearrange("p (k q) -> p k q", q=P))

                yield from attention_steps(heads, first, second, prelude)

            def run_front(b):
                yield 0
                for j in range(NT):
                    copy(front, b, f"rel{j}", relT[:, j, :], front.bank(f"rel{j}")[:, :])
                copy(front, b, "emb", xT[0:D, :], front.bank("emb")[0:D, :])
                yield 0
                copy(front, b, "nbr", xT[D:P, :], front.bank("nbr")[D:P, :], scale=w["wrd"][D:P, 0:1])
                yield 0
                yield 0
                rstd(b, 0)
                yield 0
                act.wait_ge(gate_in, b + 1)
                fn(gate[:, :, :], hid[:, :, :], ACT.Exp, scale=-1.0).then_inc(gate_exp, 1)
                yield 0
                yield 0
                copy(front, b, "silu", actT[:, :], front.bank("silu")[0:D, :])
                yield 0
                yield 0
                rstd(b, 1)
                yield 0
                copy(front, b, "ln1", lnT[:, :], front.bank("ln1")[0:D, :])
                yield 0
                copy(front, b, "comp", compT[:, :], front.bank("comp")[:, :])
                yield 0
                copy(front, b, "v", val[:, :, :], front.bank("v")[:, 0:NT * D].rearrange("p (t n) -> p t n", n=D))
                yield 0
                yield 0
                yield from attend(front, b, 1, None, front_max, front_inverse, front_norm)
                yield 0
                rstd(b, 2)
                yield 0
                copy(front, b, "ln2", lnT[:, :], front.bank("ln2")[0:D, :])
                yield 0
                for m in range(4):
                    copy(front, b, f"qpk{m}", qpkT[:, m, :], front.bank(f"qpk{m}")[:, :])
                yield 0
                for t in range(NT):
                    for s in range(2):
                        copy(front, b, f"sim{t},{s}", sim[:, t, s * 512:(s + 1) * 512], front.bank(f"sim{t},{s}")[:, :])
                    yield 0

            def run_ranks(b, t, need=0):
                for k in range(TOP_STEPS):
                    if k == HOTS_AT + 1:
                        act.wait_ge(fin_ready, b * NT + t + 1)
                        fn(fin[:, :, :], fin[:, :, :], ACT.Exp).then_inc(fin_exp, 1)
                    here = slice(t * P, (t + 1) * P)
                    if k == HOTS_AT + DH + 1:
                        ranks.wait_full(act, b, f"log{t}")
                        fn(parts[0][:, :, here], logs_of(t), ACT.Copy).then_inc(high_done, 1)
                    if k == HOTS_AT + DH + 2:
                        ranks.wait_free(act, b, f"log{t}")
                        fn(parts[1][:, :, here], rest[:, :, :], ACT.Copy).then_inc(mid_done, 1)
                        if t == NT - 1:
                            for hd in range(DH):
                                copy(ranks, b, f"stair{hd}", stairT[:, hd, :], ranks.bank(f"stair{hd}")[:, :])
                    yield need if k == HOTS_AT + DH - 1 else 0

            def kept(c):
                if not is_first(c):
                    act.wait_ge(mid_ready, c)
                    fn(lnT_cur[:, :], lnT_mid[:, :], ACT.Copy).then_inc(cur_ready, 1)
                    act.wait_ge(cur_ready, c)
                if not is_over(c):
                    front.wait_free(act, c, "ln2")
                    fn(lnT_mid[:, :], lnT[:, :], ACT.Copy).then_inc(mid_ready, 1)
                    act.wait_ge(mid_ready, c + 1)
                yield 0

            def run_back(c):
                def fetch(h, what):
                    if what == "q":
                        copy(back, c, f"q{h}", qhT[h % 2][:, :], back.bank(f"q{h}")[0:D, :], scale=D ** -0.5)
                    else:
                        copy(back, c, f"k{h}", khT[h % 2][:, :], back.bank(f"k{h}")[0:D, :])

                yield from attend(back, c, H, fetch, back_max, back_inverse, back_norm)

            def run_dense(c):
                for n in range(DH * NCHUNK + 3):
                    hd, m = divmod(n, NCHUNK)
                    v = n - 2
                    headed = v > 0 and v % NCHUNK == 0
                    done = v // NCHUNK - 1
                    if headed:
                        copy(dense, c, f"acc{done}", kvT[:, :], dense.bank(f"acc{done}")[:, :])
                    if n < DH * NCHUNK:
                        if n >= 3:
                            act.wait_ge(block_used, c * DH * NCHUNK + n - 2)
                        dense.wait_full(act, c, f"L{hd},{m}")
                        fn(dprob[n % 3][:, :], dense.bank(f"L{hd},{m}")[:, :], ACT.Exp).then_inc(dense.free(f"L{hd},{m}"), 1)
                    if headed:
                        dense.wait_full(act, c, f"kv{done}")
                        if not is_first(c):
                            act.wait_ge(kv_ready, c)
                        for t in range(NT):
                            last = fn(kv[:, t, done, :], dense.bank(f"kv{done}")[:, t * P:(t + 1) * P], ACT.Copy, scale=inv[:, t, done:done + 1])
                        last.then_inc(dense.free(f"kv{done}"), 1)
                    yield 0

            def keep_kv(c):
                act.wait_ge(slot_free, c * TILES + TILES + SLOTS)
                dense.wait_free(act, c, f"kv{DH - 1}")
                if not is_first(c):
                    back.wait_full(act, c - 1, "out")
                fn(kv_cur[:, :, :, :], kv[:, :, :, :], ACT.Copy).then_inc(kv_ready, 1)

            load_weights(act, order[1::2])
            act.wait_ge(weights_in, NW)
            drain(run_front(0))
            def scale(c, g):
                t, h = place(c, g)
                if h == DH:
                    act.wait_ge(parts_ready, c * NT + t + 1)
                act.wait_ge(rows_in[g % SLOTS], (c * (TILES // SLOTS) + g // SLOTS + 1) * 16 * TOPK)
                for s in range(TOPK):
                    at = (h - DH) * TOPK + s
                    last = fn(rows[:, g % SLOTS, s, :], rows[:, g % SLOTS, s, :], ACT.Copy, scale=wgt[:, t, at:at + 1])
                last.then_inc(scaled, 1)

            def body(c):
                if not is_first(c):
                    keep_kv(c - 1)
                weave(c, body_steps(c, run_front, run_dense, run_ranks, run_back, kept), scale, lambda c, g: None)

            drain(run_ranks(0, 0))
            body(0)
            with act.Fori(1, NB - 1) as c:
                body(c)
            body(NB - 1)

        @block.vector
        def _(dve):
            V = nc.vector
            steps = [0]

            def mark(ins):
                steps[0] += 1
                ins.then_inc(vec, 1)
                return steps[0]

            def wait(n):
                dve.wait_ge(vec, n)

            def done(ins):
                wait(mark(ins))

            def section_end():
                wait(steps[0])
                hold(dve, dve_holds)
                dve.sem_clear(vec)
                steps[0] = 0

            def over(a, n):
                return a.unsqueeze(len(a.shape)).to_broadcast(list(a.shape) + [n])

            def tiles(a):
                return a.unsqueeze(1).to_broadcast([P, NT, D])

            def grid(step):
                return front.bank(step)[:, 0:NT * D].rearrange("p (t n) -> p t n", n=D)

            def normalise(b, n, src, dst):
                done(V.tensor_reduce(stat[:, 0, :], src, AX.X, ALU.add))
                done(V.tensor_scalar(stat[:, 0, :], stat[:, 0, :], 1.0 / D, None, ALU.mult))
                done(V.tensor_tensor(dst, src, over(stat[:, 0, :], D), ALU.subtract))
                done(V.tensor_tensor(sq[:, :, :], dst, dst, ALU.mult))
                done(V.tensor_reduce(stat[:, 1, :], sq[:, :, :], AX.X, ALU.add))
                V.tensor_scalar(stat[:, 1, :], stat[:, 1, :], 1.0 / D, EPS, ALU.mult, ALU.add).then_inc(var_ready, 1)
                yield 0
                dve.wait_ge(rstd_ready, b * 3 + n + 1)

            def attend(ph, b, heads, norm_max, inverse):
                N = heads * NT

                def maxima(n):
                    h, i = divmod(n, NT)
                    step = f"S{h},{i}"
                    S = ph.bank(step)
                    ph.wait_full(dve, b, step)
                    if n >= 2:
                        ph.wait_free(dve, b, "S%d,%d" % divmod(n - 2, NT))
                    V.tensor_reduce(negmax[:, i % 2:i % 2 + 1], S[:, 0:(i + 1) * P], AX.X, ALU.max, negate=True).then_inc(norm_max, 1)

                def first(n):
                    if n + 1 < N:
                        maxima(n + 1)

                def second(n):
                    if n < N:
                        h, i = divmod(n, NT)
                        j = i % 2
                        ph.wait_free(dve, b, f"S{h},{i}")
                        V.reciprocal(pinv[:, j:j + 1], psum[:, j:j + 1]).then_inc(inverse, 1)

                yield from attention_steps(heads, first, second, lambda: maxima(0))

            def run_front(b):
                dve.wait_ge(rel_in, b * 16 + 16)
                dve.wait_ge(adj_in, b * 16 + 16)
                for t in range(NT):
                    own = rel[:, t, t * P:(t + 1) * P]
                    n = mark(V.tensor_tensor(own, own, w["noteye"][:, :], ALU.mult))
                wait(n)
                for t in range(NT):
                    last = V.tensor_tensor(rel[:, t, :], rel[:, t, :], adj[:, t, :], ALU.mult)
                last.then_inc(rel_masked, 1)
                for _ in range(3):
                    yield 0
                front.wait_full(dve, b, "h")
                if not is_first(b):
                    front.wait_full(dve, b - 1, "ln2")
                V.tensor_tensor(gate[:, :, :], grid("h"), tiles(w["b1"][:, :]), ALU.add).then_inc(front.free("h"), 1)
                front.wait_free(dve, b, "h")
                yield from normalise(b, 0, gate[:, :, :], hid[:, :, :])
                done(V.tensor_tensor(hid[:, :, :], hid[:, :, :], over(stat[:, 3, :], D), ALU.mult))
                done(V.tensor_tensor(hid[:, :, :], hid[:, :, :], tiles(w["gamma"][:, :]), ALU.mult))
                V.tensor_tensor(hid[:, :, :], hid[:, :, :], tiles(w["beta"][:, :]), ALU.add).then_inc(gate_in, 1)
                yield 0
                yield 0
                dve.wait_ge(gate_exp, b + 1)
                done(V.tensor_scalar(gate[:, :, :], gate[:, :, :], 1.0, None, ALU.add))
                done(V.reciprocal(gate[:, :, :], gate[:, :, :]))
                V.tensor_tensor(hid[:, :, :], hid[:, :, :], gate[:, :, :], ALU.mult).then_inc(silu_ready, 1)
                yield 0
                yield 0
                front.wait_full(dve, b, "tok")
                V.tensor_tensor(tok[:, :, :], grid("tok"), tiles(w["b2"][:, :]), ALU.add).then_inc(front.free("tok"), 1)
                front.wait_free(dve, b, "tok")
                front.wait_full(dve, b, "silu")
                yield from normalise(b, 1, tok[:, :, :], hid[:, :, :])
                V.tensor_tensor(hid[:, :, :], hid[:, :, :], over(stat[:, 3, :], D), ALU.mult).then_inc(ln_ready, 1)
                yield 0
                yield 0
                yield 0
                for dst, a, s, cos, sin in ((qT, "qA", "qB", "cosq", "sinq"), (kT, "kA", "kB", "cosk", "sink")):
                    front.wait_full(dve, b, a)
                    V.tensor_tensor(ropeA[:, :], front.bank(a)[0:D, :], w[cos][:, :], ALU.mult).then_inc(front.free(a), 1)
                    front.wait_full(dve, b, s)
                    V.tensor_tensor(ropeB[:, :], front.bank(s)[0:D, :], w[sin][:, :], ALU.mult).then_inc(front.free(s), 1)
                    front.wait_free(dve, b, a)
                    front.wait_free(dve, b, s)
                    if dst is qT:
                        done(V.tensor_tensor(dst[:, :], ropeA[:, :], ropeB[:, :], ALU.add))
                    else:
                        V.tensor_tensor(dst[:, :], ropeA[:, :], ropeB[:, :], ALU.add).then_inc(qk_ready, 1)
                yield 0
                yield 0
                yield from attend(front, b, 1, front_max, front_inverse)
                front.wait_full(dve, b, "att")
                V.tensor_tensor(tok[:, :, :], grid("att"), tok[:, :, :], ALU.add).then_inc(front.free("att"), 1)
                front.wait_free(dve, b, "att")
                front.wait_full(dve, b, "ln1")
                yield from normalise(b, 2, tok[:, :, :], hid[:, :, :])
                V.tensor_tensor(hid[:, :, :], hid[:, :, :], over(stat[:, 3, :], D), ALU.mult).then_inc(ln_ready, 1)
                for _ in range(6):
                    yield 0

            def top(b, t, need=0):
                front.wait_free(dve, b, f"sim{t},0")
                front.wait_free(dve, b, f"sim{t},1")
                if t or not is_first(b):
                    dve.wait_ge(hot_used, b * NT * DH + t * DH)
                done(V.tensor_copy(fsum[:, 0, :], sim[:, t, 0:H]))

                def first8(lanes, src, vals):
                    return [mark(V.max(vals(r)[:, 0:8], src(r))) for r in lanes]

                def index8(lanes, src, vals, inds, lo, m):
                    for n, r in enumerate(lanes):
                        wait(m[n])
                        m[n] = mark(V.max_index(inds(r)[:, lo:lo + 8], vals(r)[:, lo:lo + 8], src(r)))

                def drop8(lanes, src, vals, lo, m):
                    for n, r in enumerate(lanes):
                        wait(m[n])
                        m[n] = mark(V.match_replace(src(r), vals(r)[:, lo:lo + 8], src(r), LOW))

                def second8(lanes, src, vals, m):
                    for n, r in enumerate(lanes):
                        wait(m[n])
                        m[n] = mark(V.max(vals(r)[:, 8:16], src(r)))

                S, B, I = (lambda r: sim[:, t, r * NK:(r + 1) * NK]), (lambda r: best[:, r, :]), (lambda r: besti[:, r, :])
                m = first8(range(LANES), S, B)
                yield 0
                index8(range(LANES), S, B, I, 0, m)
                for hd in range(DH):
                    m.append(mark(V.tensor_tensor(
                        logs[:, hd, :, :], sim[:, t, :].rearrange("p (s h k) -> p s h k", s=2, h=H)[:, :, hd, :],
                        over(best[:, :, 0].rearrange("p (s h) -> p s h", s=2)[:, :, hd], NK), ALU.subtract)))
                wait(m[-1])
                yield 0
                drop8(range(LANES), S, B, 0, m)
                second8(range(LANES), S, B, m)
                yield 0
                index8(range(LANES), S, B, I, 8, m)
                wait(m[LANES - 1])
                mark(V.tensor_copy(bestf[:, 0:H, :], besti[:, 0:H, :]))
                mark(V.tensor_copy(best16[:, :, :, :], besti[:, :, :].rearrange("p (s h) k -> p s h k", s=2)[:, :, 0:DH, :]))
                done(V.tensor_scalar(bestf[:, H:LANES, :], besti[:, H:LANES, :], float(NK), None, ALU.mult))
                at = 0
                for a, na, nb in STAIR:
                    for src, dst in ((best, cand), (bestf, candi)):
                        n = mark(V.tensor_tensor(
                            dst[:, :, at:at + na * nb].rearrange("p h (a b) -> p h a b", b=nb),
                            src[:, 0:H, a:a + na].unsqueeze(3).to_broadcast([P, H, na, nb]),
                            src[:, H:LANES, 0:nb].unsqueeze(2).to_broadcast([P, H, na, nb]), ALU.add))
                    at += na * nb
                wait(n)
                yield 0
                C, F, G = (lambda h: cand[:, h, :]), (lambda h: fin[:, h, :]), (lambda h: finp[:, h, :])
                gh = range(DH, H)
                m = first8(range(H), C, F)
                index8(gh, C, F, G, 0, m[DH:])
                drop8(range(H), C, F, 0, m)
                second8(range(H), C, F, m)
                index8(gh, C, F, G, 8, m[DH:])
                drop8(range(DH), C, F, 8, m)
                wait(steps[0])
                yield 0
                mark(V.tensor_copy(finf[:, DH:H, :], finp[:, DH:H, :]))
                mark(V.tensor_copy(fsum[:, 0, :], fin[:, :, 0]))
                done(V.tensor_scalar(picked[:, :, :], cand[:, 0:DH, :], LOW, None, ALU.is_le))
                V.tensor_tensor(fin[:, :, :], fin[:, :, :], over(fsum[:, 0, :], TOPK), ALU.subtract).then_inc(fin_ready, 1)
                at = 0
                for a, na, nb in STAIR:
                    with nc.allow_low_precision(reason="counts up to 16"):
                        n = mark(V.tensor_reduce(worth[:, :, 0, a:a + na], picked[:, :, at:at + na * nb].rearrange("p h (a b) -> p h a b", b=nb), AX.X, ALU.add))
                    at += na * nb
                wait(n)
                for hd in range(DH):
                    hots4 = hots[hd].rearrange("p (s k) a -> p s k a", s=2)
                    done(V.tensor_tensor(hots4, key_at[:, :, :].unsqueeze(1).to_broadcast([P, 2, NK, TOPK]),
                                         best16[:, :, hd, :].unsqueeze(2).to_broadcast([P, 2, NK, TOPK]), ALU.is_equal))
                    last = V.tensor_tensor(hots4, hots4, worth[:, hd, :, :].unsqueeze(2).to_broadcast([P, 2, NK, TOPK]), ALU.mult)
                    last.then_inc(hot_ready, 1)
                    yield need if hd == DH - 1 else 0
                here = slice(t * P, (t + 1) * P)
                for h in range(DH, H, 2):
                    if h == DH + 2:
                        dve.wait_ge(high_done, b * NT + t + 1)
                        V.tensor_tensor(rest[:, :, :], logs_of(t), parts[0][:, :, here], ALU.subtract).then_inc(ranks.free(f"log{t}"), 1)
                    lane = hot[:, :, :].rearrange("p (h s) n -> p h s n", h=2)
                    done(V.tensor_tensor(hot[:, :, :], over(finf[:, h:h + 2, :].rearrange("p h s -> p (h s)"), NC),
                                         w["iota"][:, 0:NC].unsqueeze(1).to_broadcast([P, 2 * TOPK, NC]), ALU.is_equal))
                    done(V.tensor_tensor(lane, lane, candi[:, h:h + 2, :].unsqueeze(2).to_broadcast([P, 2, TOPK, NC]), ALU.mult))
                    done(V.tensor_reduce(bestf[:, h:h + 2, :].rearrange("p h s -> p (h s)"), hot[:, :, :], AX.X, ALU.add))
                    at = (h - DH) * TOPK
                    V.tensor_tensor(idx[:, t, at:at + 2 * TOPK], bestf[:, h:h + 2, :].rearrange("p h s -> p (h s)"),
                                    w["head_base"][:, h * TOPK:(h + 2) * TOPK], ALU.add).then_inc(idx_ready, 1)
                    yield 0
                dve.wait_ge(fin_exp, b * NT + t + 1)
                done(V.tensor_reduce(fsum[:, 0, :], fin[:, :, :], AX.X, ALU.add))
                done(V.reciprocal(fsum[:, 1, :], fsum[:, 0, :]))
                mark(V.tensor_copy(inv[:, t, :], fsum[:, 1, 0:DH]))
                done(V.tensor_tensor(wgt[:, t, :].rearrange("p (h s) -> p h s", h=GH), fin[:, DH:H, :], over(fsum[:, 1, DH:H], TOPK), ALU.mult))
                dve.wait_ge(mid_done, b * NT + t + 1)
                V.tensor_tensor(parts[2][:, :, here], rest[:, :, :], parts[1][:, :, here], ALU.subtract).then_inc(parts_ready, 1)
                dve.wait_ge(parts_ready, b * NT + t + 1)
                yield 0

            def run_dense(c):
                for n in range(DH * NCHUNK + 3):
                    if 1 <= n <= DH * NCHUNK:
                        hd, m = divmod(n - 1, NCHUNK)
                        at = dprob[(n - 1) % 3]
                        dense.wait_full(dve, c, f"D{hd},{m}")
                        dense.wait_free(dve, c, f"L{hd},{m}")
                        V.scalar_tensor_tensor(at[:, :], dense.bank(f"D{hd},{m}")[:, :], float(TOPK) + 0.5, at[:, :],
                                               ALU.is_gt, ALU.mult).then_inc(dense.free(f"D{hd},{m}"), 1)
                    yield 0

            def combine(c, g):
                t, h = place(c, g)
                if g == 0 and not is_first(c):
                    dve.wait_ge(kv_ready, c)
                dve.wait_ge(scaled, c * TILES + g + 1)
                V.tensor_reduce(kv[:, t, h, :], rows[:, g % SLOTS, :, :].rearrange("p s n -> p n s"), AX.X, ALU.add).then_inc(slot_free, 1)

            def kept(c):
                if not is_first(c):
                    V.tensor_copy(tok_cur[:, :, :], tok_mid[:, :, :]).then_inc(tok_ready, 1)
                    dve.wait_ge(tok_ready, c)
                if not is_over(c):
                    done(V.tensor_copy(tok_mid[:, :, :], tok[:, :, :]))
                yield 0

            def run_back(c):
                yield from attend(back, c, H, back_max, back_inverse)
                back.wait_full(dve, c, "out")
                dve.wait_ge(y_out, c * 16 + 16)
                V.tensor_copy(y[:, :, :], back.bank("out")[:, 0:NT * D].rearrange("p (t n) -> p t n", n=D)).then_inc(back.free("out"), 1)

            def body(c):
                weave(c, body_steps(c, run_front, run_dense, top, run_back, kept), lambda c, g: None, combine)
                section_end()

            V.memset(y[:, :, :], 0.0).then_inc(slot_free, SLOTS)
            dve.wait_ge(weights_in, NW)
            mark(V.tensor_copy(ident16[:, :], w["ident"][:, :]))
            mark(V.tensor_copy(key_at[:, :, :], over(w["iota"][:, :], TOPK)))
            for hd in range(DH):
                mark(V.tensor_scalar(worth[:, hd, 1, :], w["iota"][:, 0:TOPK], -1.0, float(TOPK), ALU.mult, ALU.add))
            wide_spread = spread[:, :, :].rearrange("p m (j i) -> p (m j) i", i=NK)
            mark(V.tensor_copy(wide_spread[0:NK, :, :], w["ident"][0:NK, 0:NK].unsqueeze(1).to_broadcast([NK, NK, NK])))
            mark(V.tensor_copy(wide_spread[NK:P, :, :], over(w["ident"][NK:P, NK:P], NK)))
            for _ in run(run_front(0), top(0, 0)):
                pass
            section_end()
            body(0)
            with dve.Fori(1, NB - 1) as c:
                body(c)
            body(NB - 1)


def kernel(**inputs):
    import numpy as np
    import concourse.bacc as bacc
    from concourse.bass_utils import run_bass_kernel_spmd as run

    f = np.float32
    a = {k: np.asarray(v) for k, v in inputs.items()}

    def rep(v):
        return np.ascontiguousarray(np.broadcast_to(v.reshape(1, -1), (P, v.size)))

    n_rope = D // 4
    rot = np.arange(n_rope) ^ 1
    half = n_rope // 2
    theta = (f(1.0) / (f(10000.0) ** (np.arange(half, dtype=f) / f(half)))).astype(f)
    angle = np.arange(T, dtype=f)[:, None] * theta[None, :]
    cos, sin = np.ones((D, T), f), np.zeros((D, T), f)
    cos[D - n_rope:] = np.repeat(np.cos(angle).T, 2, axis=0)
    sin[D - n_rope:] = np.repeat(np.sin(angle).T, 2, axis=0)
    sin[D - n_rope::2] *= f(-1.0)
    scale = f(D ** -0.5)
    pk = a["L0_ffn_pk_keys"]
    keys = np.zeros((4, P, 4, NK), f)
    for s in range(2):
        for h in range(H):
            keys[2 * s + h // 4, (h % 4) * 32:(h % 4 + 1) * 32, h % 4, :] = pk[s, :, h, :].T
    d = {
        "x": a["x"].view(np.uint32).reshape(NB, NT, P).transpose(0, 2, 1), "adj": a["mask_BSS_b0_1"], "rel": a["fside_BSS_rel_dist"],
        "embed": np.concatenate([a["L0_tok_atom_embed"], a["L0_tok_neighbor_embed"]], axis=1),
        "table": np.concatenate([a["L0_ffn_keys_table"], a["L0_ffn_values_table"]], axis=1),
        "ident": np.eye(P, dtype=f), "noteye": (1 - np.eye(P)).astype(f),
        "causal": np.triu(np.full((P, P), LOW, f), 1),
        "iota": rep(np.arange(NK, dtype=f)), "head_base": rep(np.repeat(np.arange(H, dtype=f) * NK * NK, TOPK)),
        "cosq": cos * scale, "sinq": sin * scale, "cosk": cos, "sink": sin,
        "wrd": a["L0_tok_w_rd"].reshape(D, 1), "w1": a["L0_tok_w1"], "b1": rep(a["L0_tok_b1"]),
        "gamma": rep(a["L0_tok_gamma"]), "beta": rep(a["L0_tok_beta"]), "w2": a["L0_tok_w2"], "b2": rep(a["L0_tok_b2"]),
        "wcomp": np.concatenate([a["L0_attn_Wq_comp"], a["L0_attn_Wkv_comp"]], axis=1),
        "wq_a": np.concatenate([a["L0_attn_Wqc"], a["L0_attn_Wqr"]], axis=1),
        "wq_b": np.concatenate([a["L0_attn_Wqc"], a["L0_attn_Wqr"][:, rot]], axis=1),
        "wk_a": np.concatenate([a["L0_attn_Wkc"], a["L0_attn_Wkr"]], axis=1),
        "wk_b": np.concatenate([a["L0_attn_Wkc"], a["L0_attn_Wkr"][:, rot]], axis=1),
        "wv": a["L0_attn_Wv"], "wpk": a["L0_ffn_Wq_pk"], "wq": a["L0_ffn_Wq"],
        "keys": keys.transpose(1, 0, 2, 3).reshape(P, 4 * 4 * NK),
        "wo": a["L0_ffn_Wo"].reshape(H, D, D).transpose(1, 0, 2).reshape(D, H * D),
    }
    d = {k: np.ascontiguousarray(v) for k, v in d.items()}
    nc = bacc.Bacc("TRN2", target_bir_lowering=False, num_devices=1)
    aps = {k: nc.dram_tensor("in_" + k, v.shape, mybir.dt.from_np(v.dtype), kind="ExternalInput").ap() for k, v in d.items()}
    out = nc.dram_tensor("out", (NB, T, D), F32, kind="ExternalOutput").ap()
    tower(nc, aps, out)
    r = run(nc, [{"in_" + k: v for k, v in d.items()}], core_ids=[0])
    return r.results[0]["out"]
```
